# Optimizing a Trainium2 kernel written in Bass

```python
import numpy as np
import jax
import jax.numpy as jnp

def _softmax(x, axis=-1):
    return jax.nn.softmax(x, axis=axis)

def _gelu(x):
    return jax.nn.gelu(x, approximate=True)

def _silu(x):
    return jax.nn.silu(x)

def _sigmoid(x):
    return jax.nn.sigmoid(x)

def _layernorm(x, axis=-1, eps=1e-05):
    m = jnp.mean(x, axis=axis, keepdims=True)
    v = jnp.var(x, axis=axis, keepdims=True)
    return (x - m) / jnp.sqrt(v + eps)

def _scatter_add(tgt, idx, src, axis=0):
    return tgt.at[idx].add(src)

def _segment_sum(src, seg, n):
    return jax.ops.segment_sum(src, seg, n)
kernel_name = 'mk_sandwich_d1_jaxref_r8_cbb9bd'

def setup_inputs(seed: int=0):
    np.random.seed(seed)
    _w = jnp.asarray

    def _L0_attn_setup():
        import jax, jax.numpy as jnp
        import numpy as np
        B, S, E, H = (2, 256, 512, 32)
        D = E // H
        ROPE_BASE = 10000.0
        MASK_VAL = -66504.0

        def _rope(x, cos, sin):
            x1, x2 = jnp.split(x, 2, axis=-1)
            return jnp.concatenate([x1 * cos - x2 * sin, x2 * cos + x1 * sin], axis=-1)
        key = jax.random.key(seed)
        k1, k2, k3, k4, k5 = jax.random.split(key, 5)
        return {'hidden_states': jax.random.normal(k1, (B, S, E), dtype=jnp.float32), 'qkv_w': jax.random.normal(k2, (E, 3 * E), dtype=jnp.float32) * 0.02, 'qkv_b': jax.random.normal(k3, (3 * E,), dtype=jnp.float32) * 0.02, 'out_w': jax.random.normal(k4, (E, E), dtype=jnp.float32) * 0.02, 'out_b': jax.random.normal(k5, (E,), dtype=jnp.float32) * 0.02}
    _L0_attn_in = _L0_attn_setup()

    def _L0_ffn_setup():
        import jax, jax.numpy as jnp
        import numpy as np
        H = 512
        I = 256
        E = 16
        TOPK = 4
        SI = 256
        key = jax.random.key(seed)
        ks = jax.random.split(key, 9)
        s = 0.02
        return {'hidden_states': jax.random.normal(ks[0], (2, 256, H), dtype=jnp.float32), 'gate_w': jax.random.normal(ks[1], (E, H), dtype=jnp.float32) * s, 'bias': jnp.zeros((E,), dtype=jnp.float32), 'Wg': jax.random.normal(ks[2], (E, I, H), dtype=jnp.float32) * s, 'Wu': jax.random.normal(ks[3], (E, I, H), dtype=jnp.float32) * s, 'Wd': jax.random.normal(ks[4], (E, H, I), dtype=jnp.float32) * s, 'Sg': jax.random.normal(ks[5], (SI, H), dtype=jnp.float32) * s, 'Su': jax.random.normal(ks[6], (SI, H), dtype=jnp.float32) * s, 'Sd': jax.random.normal(ks[7], (H, SI), dtype=jnp.float32) * s}
    _L0_ffn_in = _L0_ffn_setup()
    _d = {'L0_attn_hidden_states': _L0_attn_in['hidden_states'], 'L0_attn_qkv_w': _L0_attn_in['qkv_w'], 'L0_attn_qkv_b': _L0_attn_in['qkv_b'], 'L0_attn_out_w': _L0_attn_in['out_w'], 'L0_attn_out_b': _L0_attn_in['out_b'], 'L0_ffn_gate_w': _L0_ffn_in['gate_w'], 'L0_ffn_bias': _L0_ffn_in['bias'], 'L0_ffn_Wg': _L0_ffn_in['Wg'], 'L0_ffn_Wu': _L0_ffn_in['Wu'], 'L0_ffn_Wd': _L0_ffn_in['Wd'], 'L0_ffn_Sg': _L0_ffn_in['Sg'], 'L0_ffn_Su': _L0_ffn_in['Su'], 'L0_ffn_Sd': _L0_ffn_in['Sd']}
    _x0 = _d['L0_attn_hidden_states']
    _d['L0_attn_hidden_states'] = jax.random.normal(jax.random.fold_in(jax.random.key(seed), 1), (2, 512, 512), dtype=_x0.dtype)
    del _x0
    return _d

def reference(L0_attn_hidden_states, L0_attn_qkv_w, L0_attn_qkv_b, L0_attn_out_w, L0_attn_out_b, L0_ffn_gate_w, L0_ffn_bias, L0_ffn_Wg, L0_ffn_Wu, L0_ffn_Wd, L0_ffn_Sg, L0_ffn_Su, L0_ffn_Sd):

    def _L0_attn_ref(hidden_states, qkv_w, qkv_b, out_w, out_b):
        import jax, jax.numpy as jnp
        import numpy as np
        B, S, E, H = (2, 256, 512, 32)
        D = E // H
        ROPE_BASE = 10000.0
        MASK_VAL = -66504.0

        def _rope(x, cos, sin):
            x1, x2 = jnp.split(x, 2, axis=-1)
            return jnp.concatenate([x1 * cos - x2 * sin, x2 * cos + x1 * sin], axis=-1)
        b, s, e = hidden_states.shape
        qkv = hidden_states @ qkv_w + qkv_b
        q, k, v = jnp.split(qkv, 3, axis=-1)
        q = q.reshape(b, s, H, D)
        k = k.reshape(b, s, H, D)
        v = v.reshape(b, s, H, D)
        half = D // 2
        inv_freq = 1.0 / ROPE_BASE ** (jnp.arange(0, half, dtype=jnp.float32) / half)
        ang = jnp.arange(s, dtype=jnp.float32)[:, None] * inv_freq[None, :]
        cos = jnp.cos(ang)[None, :, None, :]
        sin = jnp.sin(ang)[None, :, None, :]
        q = _rope(q, cos, sin)
        k = _rope(k, cos, sin)
        scale = 1.0 / jnp.sqrt(jnp.asarray(D, dtype=hidden_states.dtype))
        scores = jnp.einsum('bqhd,bkhd->bhqk', q, k) * scale
        causal = jnp.tril(jnp.ones((s, s), dtype=scores.dtype))
        scores = scores + (1.0 - causal) * MASK_VAL
        probs = jax.nn.softmax(scores, axis=-1)
        ctx = jnp.einsum('bhqk,bkhd->bqhd', probs, v).reshape(b, s, e)
        return ctx @ out_w + out_b

    def _L0_ffn_ref(hidden_states, gate_w, bias, Wg, Wu, Wd, Sg, Su, Sd):
        import jax, jax.numpy as jnp
        import numpy as np
        H = 512
        I = 256
        E = 16
        TOPK = 4
        SI = 256
        orig_shape = hidden_states.shape
        x = hidden_states.reshape(-1, orig_shape[-1])
        scores = jax.nn.sigmoid(x @ gate_w.T) + bias
        topk_w, topk_idx = jax.lax.top_k(scores, TOPK)
        topk_w = topk_w / (jnp.sum(topk_w, axis=-1, keepdims=True) + 1e-20)
        cw = jnp.sum(jax.nn.one_hot(topk_idx, E, dtype=x.dtype) * topk_w[..., None], axis=1)
        g = jnp.einsum('th,eih->eti', x, Wg)
        u = jnp.einsum('th,eih->eti', x, Wu)
        z = jax.nn.silu(g) * u
        zw = z * cw.T[:, :, None]
        out = jnp.einsum('eti,ehi->th', zw, Wd)
        out = out + jax.nn.silu(x @ Sg.T) * (x @ Su.T) @ Sd.T
        return out.reshape(orig_shape)
    x = L0_attn_hidden_states
    x = x + _layernorm(_L0_attn_ref(_layernorm(x, axis=-1), L0_attn_qkv_w, L0_attn_qkv_b, L0_attn_out_w, L0_attn_out_b), axis=-1)
    x = x + _layernorm(_L0_ffn_ref(_layernorm(x, axis=-1), L0_ffn_gate_w, L0_ffn_bias, L0_ffn_Wg, L0_ffn_Wu, L0_ffn_Wd, L0_ffn_Sg, L0_ffn_Su, L0_ffn_Sd), axis=-1)
    return x

_drawn_inputs = setup_inputs


def setup_inputs(seed=0):
    import zlib

    import numpy as np

    out = dict(_drawn_inputs(seed))
    spreads = {'L0_ffn_bias': (0.0, 0.1)}
    factors = {}
    for name, (base, spread) in spreads.items():
        noise = np.random.default_rng([zlib.crc32(name.encode()), seed]).standard_normal(out[name].shape)
        drawn = base * np.exp(spread * noise) if base else spread * noise
        out[name] = jnp.asarray(drawn.astype(out[name].dtype))
    for name, factor in factors.items():
        out[name] = (out[name] * factor).astype(out[name].dtype)
    return out
```

```python
from contextlib import ExitStack

import concourse.bass as bass
from concourse import mybir

F32 = mybir.dt.float32
F32R = mybir.dt.float32r
BF16 = mybir.dt.bfloat16
I32 = mybir.dt.int32
U32 = mybir.dt.uint32
ALU = mybir.AluOpType
ACT = mybir.ActivationFunctionType
AX = mybir.AxisListType

P = 128
B, S, E = 2, 512, 512
H, D = 32, 16
T = B * S
NT = T // P
TB = S // P
KE = E // P
NP = B * H // 2
STK = 64
NX, TOPK, FI = 16, 4, 256
KF = FI // P
MAXT = T * TOPK // P + NX - 1
TT = 64
EPS = 1e-5
MASKED_BITS = 0xC782
ONE_BITS = 0x3F80
WSLOT = 3 * KE * FI
RING = 4


def build(nc, x, qkv_w, qkv_b, out_w, out_b, gate, ebias, wg, sg, sd,
          ident, mask, tri, rope, fill, tok, less, steps, out):
    ctx = ExitStack()
    with ctx:
        def sb(name, shape, dt=F32):
            return ctx.enter_context(nc.sbuf_tensor(name, shape, dt))

        def sem(name):
            return ctx.enter_context(nc.semaphore(name))

        bank = [ctx.enter_context(nc.psum_tensor(f"bank{i}", [P, 512], F32)) for i in range(8)]

        ident_sb = sb("ident_sb", [P, P])
        identb = sb("identb", [P, P], BF16)
        mask_sb = sb("mask_sb", [P, P], BF16)
        rope_sb = sb("rope_sb", [P, TB, 4, D])
        qkvb_sb = sb("qkvb_sb", [P, 3 * E])
        outb_sb = sb("outb_sb", [P, E])
        x_sb = sb("x_sb", [P, NT, E])
        stats = sb("stats", [P, NT, 6])
        mv = sb("mv", [P, NT, 2])
        rstd = sb("rstd", [P, NT])
        nwt = sb("nwt", [P, 2, NT])
        work = sb("work", [P, 10240])
        qkvw_sb = work[:, 0:6144].rearrange("p (k n) -> p k n", k=KE)
        xn = work[:, 6144:7168].rearrange("p (r e) -> p r e", r=2)
        xT = work[:, 7168:8192].rearrange("p (r k q) -> p r k q", r=2, k=KE)
        qkraw = work[:, 8192:10240].rearrange("p (r f h d) -> p r f h d", r=2, f=2, h=H)
        probs = work[:].rearrange("p (r u c q) -> p r u c q", r=2, u=2, c=5)
        outw_sb = sb("outw_sb", [P, KE, E])
        rot = sb("rot", [P, 2, H, D])
        big = sb("big", [P, 16384])
        qkr = big[:, 0:8192].rearrange("p (b f u t c) -> p b f u t c", b=B, f=2, u=H // 2, t=TB)
        vaug = big[:, 8192:16384].rearrange("p (t h d) -> p t h d", t=NT, h=H)
        qst = sb("qst", [P, 2, TB, 2, STK], F32R)
        kst = sb("kst", [P, 2, TB, 2, STK], F32R)
        qS = sb("qS", [P, 4, S], F32R)
        kA = sb("kA", [P, 4, S], F32R)
        kB = sb("kB", [P, 4, S], F32R)
        mneg = sb("mneg", [P, 2, 8], F32R)
        mT = sb("mT", [8, 2, P])
        cT = sb("cT", [P, 2, S])
        rsum = sb("rsum", [P, TB, 4])
        cx = sb("cx", [P, NT, E])

        s_const = sem("const_loaded")
        s_xin = [sem(f"x_loaded{b}") for b in range(B)]
        s_w = sem("qkv_weights_loaded")
        s_ow = sem("out_weights_loaded")
        s_idb = sem("identity_in_bf16")
        s_init = sem("buffers_initialised")
        dch = sem("vector_chain")
        pch = sem("pool_chain")
        s_xn = sem("xn_ready")
        s_xtr = sem("x_transposed")
        s_xT = sem("xT_ready")
        s_qkv = sem("qkv_done")
        s_raw = sem("qkv_evacuated")
        s_rot = sem("rope_sin_part_ready")
        s_rope = sem("rope_done")
        s_st = sem("stacks_ready")
        s_hi = sem("stacks_high_parts_ready")
        s_trq = sem("q_stacks_transposed")
        s_tr = sem("k_stacks_transposed")
        s_qe = sem("q_evacuated")
        s_ke = sem("kA_evacuated")
        s_kf = sem("kB_evacuated")
        s_mx = sem("max_scores_done")
        s_red = sem("max_reduced")
        s_mt = sem("max_transposed")
        s_mc = sem("max_rows_copied")
        s_md = [sem(f"max_rows_in_place{i}") for i in range(4)]
        s_sc = sem("scores_done")
        s_ex = sem("exp_done")
        s_zf = sem("masked_probs_zeroed")
        s_pv = sem("pv_done")
        s_ce = sem("ctx_evacuated")
        s_ct = sem("ctx_transposed")
        s_cx = sem("ctx_normalised")

        hT = work[:, 0:4096].rearrange("p (k t) -> p k t", k=KE)
        ctxT = work[:, 4096:5120].rearrange("p (r k q) -> p r k q", r=2, k=KE)
        sgu_sb = work[:, 5120:7168].rearrange("p (k n) -> p k n", k=KE)
        sd_sb = work[:, 7168:8192].rearrange("p (k n) -> p k n", k=KF)
        zs = work[:, 8192:10240].rearrange("p (k t) -> p k t", k=KF)
        ring = big[:, 0:RING * WSLOT]
        above = big[:, 12288:14336].rearrange("p (t e f) -> p t e f", t=NT, e=NX)
        equal = big[:, 14336:16384].rearrange("p (t e f) -> p t e f", t=NT, e=NX)
        gate_sb = sb("gate_sb", [P, KE, NX])
        ebias_sb = sb("ebias_sb", [P, NX])
        less_sb = sb("less_sb", [P, NX, NX])
        steps_sb = sb("steps_sb", [P, TT])
        tri_sb = sb("tri_sb", [P, 2, P], BF16)
        score = sb("score", [P, NT, NX])
        rank = sb("rank", [P, NT, NX])
        chosen = sb("chosen", [P, NT, NX], BF16)
        onehot = sb("onehot", [P, NT, TOPK, NX])
        pick = sb("pick", [P, NT, TOPK, NX])
        before = sb("before", [P, NT + 1, NX])
        slot = sb("slot", [P, NT, NX])
        cmp7 = sb("cmp7", [P, NX, 7])
        ntile = sb("ntile", [P, NX])
        tsum = sb("tsum", [P, NX, NX])
        tfirst = sb("tfirst", [P, NX])
        tend = sb("tend", [P, NX])
        owner = big[:, 12288:13312].rearrange("p (i e) -> p i e", i=TT)
        own = sb("own", [P, TT])
        wtop = sb("wtop", [P, NT, TOPK])
        wden = sb("wden", [P, NT])
        sl_f = sb("sl_f", [P, NT, TOPK])
        sl_i = sb("sl_i", [P, 2, NT, TOPK], U32)
        pay = sb("pay", [P, NT, TOPK, 2], I32)
        tok_sb = sb("tok_sb", [P, NT], I32)
        plan = sb("plan", [P, 2, TT], I32)
        ends = sb("ends", [P, NX + 1], I32)
        table = sb("table", [P, TT, 2], I32)
        gidx = sb("gidx", [P, 2], U32)
        smeta = sb("smeta", [P, 2, 2], I32)
        loop = big[:, 12288:16384]
        hg = loop[:, 0:1024].rearrange("p (r e) -> p r e", r=2)
        hTt = loop[:, 1024:2048].rearrange("p (r k q) -> p r k q", r=2, k=KE)
        th = loop[:, 2048:2560].rearrange("p (r f) -> p r f", r=2)
        act_z = loop[:, 2560:3072].rearrange("p (r f) -> p r f", r=2)
        z = loop[:, 3072:3584].rearrange("p (r f) -> p r f", r=2)
        zT = loop[:, 3584:4096].rearrange("p (r k q) -> p r k q", r=2, k=KF)
        y = outw_sb[:, 0:2, :]
        h_rows = nc.dram_tensor("h_rows", (T + P, E), F32).ap()
        acc = nc.dram_tensor("acc_rows", (T + P, E), F32).ap()
        slots = nc.dram_tensor("slot_table", (P * TT, 2), I32).ap()

        s_rc = sem("router_constants_loaded")
        s_ctr = sem("ctx_rows_turned")
        s_ctT = sem("ctxT_ready")
        s_op = sem("out_projected")
        s_a = sem("attention_rows_ready")
        s_h = sem("h_ready")
        s_hst = sem("h_stored")
        s_htr = sem("h_turned")
        s_hT = sem("hT_ready")
        s_lg = sem("logits_done")
        s_tanh = sem("router_tanh_done")
        s_ch = sem("chosen_ready")
        s_cnt = sem("counts_done")
        s_pay = sem("slots_ready")
        s_plan = sem("plan_ready")
        s_sct = sem("slots_scattered")
        s_tab = sem("table_loaded")
        s_sw = sem("shared_weights_loaded")
        s_sgu = sem("shared_gu_done")
        s_sth = sem("shared_tanh_done")
        s_sz = sem("shared_z_ready")
        s_sdn = sem("shared_down_done")
        s_sy = sem("shared_rows_ready")
        s_syst = [sem(f"shared_rows_stored{i}") for i in range(2)]
        s_wd = [sem(f"expert_weights_landed{i}") for i in range(RING)]
        s_wr = sem("expert_weights_ready")
        s_ga = [sem(f"rows_gathered{i}") for i in range(2)]
        s_tx = sem("rows_turned")
        s_he = sem("rows_evacuated")
        s_gu = sem("gu_done")
        s_th = sem("tanh_done")
        s_az = sem("silu_part_ready")
        s_z = sem("z_ready_plus_1")
        s_tz = sem("z_turned")
        s_zt = sem("zT_ready")
        s_dn = sem("down_done")
        s_ye = sem("y_ready_plus_3")
        s_ms = sem("slot_meta_ready")
        s_sca = sem("table_prefilled_then_y_scattered")
        s_scd = sem("scatters_seen_plus_3")
        s_gi = sem("gathers_begun")
        s_ix = sem("gather_index_ready")
        s_mdone = sem("all_scattered")
        s_acc = [sem(f"acc_loaded{i}") for i in range(2)]
        s_fin = sem("rows_final")
        s_out = sem("out_stored")

        block = ctx.enter_context(nc.Block())

        TRQ, TRK, MX, ST, PVB, MISC = bank[0], bank[1], bank[2:4], bank[4:6], bank[6], bank[7]

        def heads(u):
            return u // (NP // B), 2 * (u % (NP // B))

        @block.sync
        def _(sp):
            for b in range(B):
                sp.dma_start(x_sb[:, b * TB:(b + 1) * TB, :],
                             x[b * S:(b + 1) * S, :].rearrange("(t p) e -> p t e", p=P)).then_inc(s_xin[b], 16)
            sp.dma_start(ident_sb[:], ident).then_inc(s_const, 16)
            sp.dma_start(mask_sb[:], mask.bitcast(BF16)).then_inc(s_const, 16)
            sp.dma_start(rope_sb[:], rope.rearrange("(t p) f d -> p t f d", p=P)).then_inc(s_const, 16)
            sp.dma_start(qkvw_sb[:], qkv_w.rearrange("(k p) n -> p k n", p=P)).then_inc(s_w, 16)
            sp.dma_start(qkvb_sb[:], qkv_b.rearrange("(o n) -> o n", o=1).broadcast_to([P, 3 * E])).then_inc(s_const, 16)
            sp.dma_start(outb_sb[:], out_b.rearrange("(o n) -> o n", o=1).broadcast_to([P, E])).then_inc(s_const, 16)
            sp.dma_start(outw_sb[:], out_w.rearrange("(k p) n -> p k n", p=P)).then_inc(s_ow, 16)
            for u in range(NP):
                sp.wait_ge(s_mc, u + 1)
                for h in range(2):
                    sp.dma_start(qS[64 * h + 32:64 * h + 33, u % 4, :].bitcast(F32).rearrange("o (i q) -> o i q", q=P),
                                 mT[4 * h:4 * h + 4, u % 2, :]).then_inc(s_md[u % 4], 16)
            sp.dma_start(gate_sb[:], gate.rearrange("(k p) n -> p k n", p=P)).then_inc(s_rc, 16)
            sp.dma_start(ebias_sb[:], ebias.rearrange("(o n) -> o n", o=1).broadcast_to([P, NX])).then_inc(s_rc, 16)
            sp.dma_start(less_sb[:], less.rearrange("(o e) f -> o e f", o=1).broadcast_to([P, NX, NX])).then_inc(s_rc, 16)
            sp.dma_start(steps_sb[:], steps.rearrange("(o n) -> o n", o=1).broadcast_to([P, TT])).then_inc(s_rc, 16)
            sp.dma_start(tri_sb[:], tri.bitcast(BF16)).then_inc(s_rc, 16)
            sp.dma_start(tok_sb[:], tok).then_inc(s_rc, 16)
            sp.wait_ge(s_cx, NP // 2)
            sp.wait_ge(s_pv, NP // 2)
            sp.dma_start(sgu_sb[:], sg.rearrange("(k p) n -> p k n", p=P)).then_inc(s_sw, 16)
            sp.dma_start(sd_sb[:], sd.rearrange("(k p) n -> p k n", p=P)).then_inc(s_sw, 16)
            for e in range(RING):
                sp.dma_start(ring[:, e * WSLOT:(e + 1) * WSLOT], wg[e]).then_inc(s_wd[e], 16)
            for t in range(NT):
                sp.wait_ge(s_h, t + 1)
                sp.dma_start(h_rows[t * P:(t + 1) * P, :], cx[:, t, :]).then_inc(s_hst, 16)
                if t == 0:
                    sp.dma_start(h_rows[T:T + P, :], cx[:, t, :]).then_inc(s_hst, 16)
            for t in range(NT):
                sp.wait_ge(s_sy, t + 1)
                sp.dma_start(acc[t * P:(t + 1) * P, :], y[:, t % 2, :]).then_inc(s_syst[t % 2], 16)
                if t == 0:
                    sp.dma_start(acc[T:T + P, :], y[:, 0, :]).then_inc(s_syst[0], 16)
            sp.wait_ge(s_sct, 16 * NT * TOPK)
            sp.dma_start(table[:], slots.rearrange("(p i) c -> p i c", p=P)).then_inc(s_tab, 16)
            for e in range(RING):
                sp.wait_ge(s_wd[e], 16)
                sp.sem_inc(s_wr, 1)
            sp.wait_ge(s_plan, 1)
            for e in range(RING, NX):
                sp.wait_ge(s_dn, sp.value_load(ends[0:1, e - RING:e - RING + 1], min_val=1, max_val=MAXT))
                r = e % RING
                sp.dma_start(ring[:, r * WSLOT:(r + 1) * WSLOT], wg[e]).then_inc(s_wd[r], 16)
                sp.wait_ge(s_wd[r], 16 * (e // RING + 1))
                sp.sem_inc(s_wr, 1)
            sp.wait_ge(s_mdone, 1)
            for b in range(B):
                sp.dma_start(cx[:, b * TB:(b + 1) * TB, :],
                             acc[b * S:(b + 1) * S, :].rearrange("(t p) e -> p t e", p=P)).then_inc(s_acc[b], 16)
            for b in range(B):
                sp.wait_ge(s_fin, TB * (b + 1))
                sp.dma_start(out[b * S:(b + 1) * S, :].rearrange("(t p) e -> p t e", p=P),
                             x_sb[:, b * TB:(b + 1) * TB, :]).then_inc(s_out, 16)
            sp.wait_ge(s_out, 16 * B)

        @block.gpsimd
        def _(pool):
            n = [0]

            def link(ins):
                n[0] += 1
                ins.then_inc(pch, 1)
                pool.wait_ge(pch, n[0])

            pool.dma_start(slots, fill).then_inc(s_sca, 16)
            pool.memset(qst[:].bitcast(U32), 0)
            pool.memset(kst[:].bitcast(U32), 0)
            link(pool.memset(kA[:].bitcast(U32), 0))
            link(pool.memset(kst[:, :, :, :, 32:33].bitcast(F32), 1.0))
            link(pool.memset(vaug[:, :, :, 17:32], 0.0))
            pool.memset(vaug[:, :, :, 16:17], 1.0)
            pool.memset(kB[:].bitcast(U32), 0).then_inc(s_init, 1)
            pool.wait_ge(s_const, 80)
            for t in range(NT):
                pool.wait_ge(s_raw, 2 * t + 1)
                if t >= 1:
                    pool.wait_ge(s_rope, t)
                raw = qkraw[:, t % 2]
                for half in range(2):
                    lo, hi = 8 * half, 8 * (1 - half)
                    for f in range(2):
                        ins = pool.tensor_tensor(
                            rot[:, f, :, lo:lo + 8], raw[:, f, :, hi:hi + 8],
                            rope_sb[:, t % TB, 2 + f:3 + f, lo:lo + 8].broadcast_to([P, H, 8]), ALU.mult)
                ins.then_inc(s_rot, 1)

            def low_parts(u):
                b, h0 = heads(u)
                pool.wait_ge(s_hi, u + 1)
                for f, st, low in ((0, qst, 48), (1, kst, 16)):
                    o = st[:, u % 2].rearrange("p t h c -> p (t h) c")
                    src = qkr[:, b, f, h0 // 2].rearrange("p t (h d) -> p (t h) d", d=D)
                    ins = pool.tensor_tensor(o[:, :, low:low + 16], src, o[:, :, 0:16].bitcast(F32), ALU.subtract)
                ins.then_inc(s_st, 1)

            def zero_masked(u):
                pb = probs[:, (u // 2) % 2, u % 2]
                for c, view in ((2, pb[:, 0:2, 0:128]),
                                (3, pb[:, 2, :].rearrange("p (d q) -> p d q", q=P)[:, 0:4:3, :]),
                                (4, pb[:, 3, :].rearrange("p (d q) -> p d q", q=P)[:, 0:4:3, :]),
                                (5, pb[:, 4, :].rearrange("p (d q) -> p d q", q=P)[:, 0:4:2, :])):
                    pool.wait_ge(s_ex, 5 * u + c)
                    pat = [[0, k] for k in view.shape[1:-1]] + [[1, P]]
                    ins = pool.affine_select(out=view, in_=view, compare_op=ALU.is_ge, fill=0.0, base=0,
                                             pattern=pat, channel_multiplier=-1)
                ins.then_inc(s_zf, 1)

            low_parts(0)
            for s in range(NP + 2):
                if s + 1 < NP:
                    low_parts(s + 1)
                if s - 2 >= 0:
                    zero_masked(s - 2)

            pool.wait_ge(s_sca, 16)
            pool.wait_ge(s_pay, 1)
            for t in range(NT):
                for k in range(TOPK):
                    pool.indirect_dma_start(slots, bass.IndirectOffsetOnAxis(sl_i[:, 0, t, k:k + 1], 0),
                                            pay[:, t, k, :], None).then_inc(s_sct, 16)

            def gather(i, par, after):
                if after is not None:
                    pool.wait_ge(s_tx, after)
                pool.tensor_copy(gidx[:, par:par + 1], table[:, bass.ds(i, 1), 0].bitcast(U32)).then_inc(s_ix, 1)
                pool.wait_ge(s_ix, i + 1)
                pool.sem_inc(s_gi, 1)
                pool.indirect_dma_start(hg[:, par, :], None, h_rows,
                                        bass.IndirectOffsetOnAxis(gidx[:, par:par + 1], 0)).then_inc(s_ga[par], 16)

            def meta(j, par):
                pool.tensor_copy(smeta[:, par, :], table[:, bass.ds(j, 1), :].rearrange("p o c -> p (o c)")).then_inc(s_ms, 1)

            def scatter(j, par):
                pool.wait_ge(s_ye, j + 4)
                pool.wait_ge(s_sca, 16 * j + 16)
                pool.sem_inc(s_scd, 1)
                pool.indirect_dma_start(acc, bass.IndirectOffsetOnAxis(smeta[:, par, 0:1].bitcast(U32), 0),
                                        y[:, par, :], None, compute_op=ALU.add).then_inc(s_sca, 16)

            pool.wait_ge(s_plan, 1)
            pool.wait_ge(s_tab, 16)
            pool.wait_ge(s_hst, 16 * (NT + 1))
            pool.sem_inc(s_scd, 2)
            gather(0, 0, None)
            gather(1, 1, None)
            gather(2, 0, 1)
            pool.wait_ge(s_syst[0], 16 * (NT // 2 + 1))
            pool.wait_ge(s_syst[1], 16 * (NT // 2))
            n2 = pool.value_load(ends[0:1, NX:NX + 1], min_val=1, max_val=TT // 2 - 2)
            with pool.Fori(0, n2) as m:
                for r in range(2):
                    i = 2 * m + 1 + r
                    gather(i + 2, 1 - r, i + 1)
                    meta(i - 1, r)
                    scatter(i - 1, r)
            meta(2 * n2, 0)
            scatter(2 * n2, 0)
            pool.wait_ge(s_sca, 32 * n2 + 32)
            pool.sem_inc(s_mdone, 1)

        @block.scalar
        def _(act):
            for t in range(NT):
                act.wait_ge(s_xtr, t + 1)
                if t >= 2:
                    act.wait_ge(s_qkv, t - 1)
                act.activation(xT[:, t % 2].rearrange("p k q -> p (k q)"), bank[6 + t % 2][:], ACT.Copy).then_inc(s_xT, 1)
            act.wait_ge(s_init, 1)

            def q_evac(u):
                act.wait_ge(s_trq, u + 1)
                if u >= 4:
                    act.wait_ge(s_sc, 5 * (u - 3))
                act.activation(qS[:, u % 4, :], TRQ[:], ACT.Copy).then_inc(s_qe, 1)

            def kb_evac(u):
                act.wait_ge(s_tr, u + 1)
                if u >= 4:
                    act.wait_ge(s_sc, 5 * (u - 3))
                act.activation(kB[64:128, u % 4, :], TRK[64:128, :], ACT.Copy).then_inc(s_kf, 1)

            def max_rows(u):
                act.wait_ge(s_mt, u + 1)
                if u >= 2:
                    act.wait_ge(s_md[(u - 2) % 4], 32 * ((u - 2) // 4 + 1))
                act.activation(mT[:, u % 2, :], MISC[0:8, 0:P], ACT.Copy).then_inc(s_mc, 1)

            def exp(u, c):
                act.wait_ge(s_sc, 5 * u + c + 1)
                if c == 0 and u % 2 == 0 and u >= 4:
                    act.wait_ge(s_pv, u // 2 - 1)
                act.activation(probs[:, (u // 2) % 2, u % 2, c, :], ST[(5 * u + c) % 2][:], ACT.Exp).then_inc(s_ex, 1)

            q_evac(0)
            kb_evac(0)
            for s in range(NP + 2):
                for c in range(5):
                    if s >= 2:
                        exp(s - 2, c)
                    if c == 1 and s + 1 < NP:
                        q_evac(s + 1)
                    if c == 2 and 1 <= s <= NP:
                        max_rows(s - 1)
                    if c == 3 and s + 1 < NP:
                        kb_evac(s + 1)
            for t in range(NT):
                act.wait_ge(s_ctr, t + 1)
                if t >= 2:
                    act.wait_ge(s_op, t - 1)
                act.activation(ctxT[:, t % 2].rearrange("p k q -> p (k q)"), bank[t % 2][:], ACT.Copy).then_inc(s_ctT, 1)
            for t in range(NT):
                act.wait_ge(s_htr, t + 1)
                act.activation(hT[:, :, t * P:(t + 1) * P], bank[t % 2][:].rearrange("p (k q) -> p k q", k=KE),
                               ACT.Copy).then_inc(s_hT, 1)
            act.wait_ge(s_lg, 1)
            act.activation(score[:].rearrange("p t e -> p (t e)"), bank[4][:, 0:P], ACT.Tanh, scale=0.5).then_inc(s_tanh, 1)
            for c in range(4):
                act.wait_ge(s_sgu, c + 1)
                if c >= 2:
                    act.wait_ge(s_sz, c - 1)
                act.activation(y[:, c % 2, :], bank[2 * (c % 2)][:], ACT.Tanh, scale=0.5).then_inc(s_sth, 1)
            act.wait_ge(s_sz, 4)
            for t in range(NT):
                act.wait_ge(s_sdn, t + 1)
                if t >= 2:
                    act.wait_ge(s_syst[t % 2], 16 * (t // 2 + (t % 2 == 0)))
                act.activation(y[:, t % 2, :], bank[t % 4][:], ACT.Copy).then_inc(s_sy, 1)

            def rows_evac(i, par):
                act.wait_ge(s_tx, i + 1)
                act.activation(hTt[:, par].rearrange("p k q -> p (k q)"), bank[par][:], ACT.Copy).then_inc(s_he, 1)

            def tanh(i, par):
                act.wait_ge(s_gu, i + 1)
                act.wait_ge(s_z, i)
                act.activation(th[:, par, :], bank[2 + par][:, 0:FI], ACT.Tanh, scale=0.5).then_inc(s_th, 1)

            def y_evac(j, par):
                act.wait_ge(s_dn, j + 1)
                act.wait_ge(s_ms, j + 1)
                act.wait_ge(s_scd, j + 2)
                act.activation(y[:, par, :], bank[6 + par][:], ACT.Copy, scale=smeta[:, par, 1:2].bitcast(F32)).then_inc(s_ye, 1)

            act.wait_ge(s_syst[0], 16 * (NT // 2 + 1))
            act.wait_ge(s_syst[1], 16 * (NT // 2))
            act.sem_inc(s_ye, 3)
            act.wait_ge(s_plan, 1)
            n2 = act.value_load(ends[0:1, NX:NX + 1], min_val=1, max_val=TT // 2 - 2)
            rows_evac(0, 0)
            act.wait_ge(s_gu, 1)
            act.activation(th[:, 0, :], bank[2][:, 0:FI], ACT.Tanh, scale=0.5).then_inc(s_th, 1)
            rows_evac(1, 1)
            with act.Fori(0, n2) as m:
                for r in range(2):
                    i = 2 * m + 1 + r
                    tanh(i, 1 - r)
                    rows_evac(i + 1, r)
                    y_evac(i - 1, r)
            y_evac(2 * n2, 0)

        @block.vector
        def _(dve):
            n = [0]

            def link(ins):
                n[0] += 1
                ins.then_inc(dch, 1)
                dve.wait_ge(dch, n[0])

            def rsqrt(o, var, w):
                v, y = w
                link(dve.tensor_scalar(v, var, EPS, None, ALU.add))
                link(dve.tensor_scalar(y.bitcast(I32), v.bitcast(I32), 1, None, ALU.logical_shift_right))
                link(dve.tensor_scalar(y.bitcast(I32), y.bitcast(I32), -1.0, 1597463007.0, ALU.mult, ALU.add))
                for _ in range(4):
                    link(dve.tensor_tensor(o, y, y, ALU.mult))
                    link(dve.tensor_tensor(o, o, v, ALU.mult))
                    link(dve.tensor_scalar(o, o, -0.5, 1.5, ALU.mult, ALU.add))
                    link(dve.tensor_tensor(y, y, o, ALU.mult))
                link(dve.tensor_copy(o, y))

            for t in range(NT):
                if t % TB == 0:
                    dve.wait_ge(s_xin[t // TB], 16)
                last = dve.bn_stats(stats[:, t, :], x_sb[:, t, :])
            link(last)
            for t in range(NT):
                last = dve.bn_aggr(mv[:, t, :], stats[:, t, :])
            link(last)
            rsqrt(rstd[:], mv[:, :, 1], (nwt[:, 0, :], nwt[:, 1, :]))

            def norm(t):
                if t >= 2:
                    dve.wait_ge(s_xtr, t - 1)
                dve.tensor_scalar(xn[:, t % 2, :], x_sb[:, t, :], mv[:, t, 0:1], rstd[:, t:t + 1],
                                  ALU.subtract, ALU.mult).then_inc(s_xn, 1)

            norm(0)
            norm(1)
            dve.wait_ge(s_const, 80)
            dve.tensor_copy(identb[:], ident_sb[:]).then_inc(s_idb, 1)
            dve.wait_ge(s_init, 1)

            def bias(t):
                dve.wait_ge(s_qkv, t + 1)
                raw = qkraw[:, t % 2]
                for f in range(2):
                    ins = dve.tensor_tensor(raw[:, f], bank[3 * (t % 2) + f][:], qkvb_sb[:, f * E:(f + 1) * E], ALU.add)
                ins.then_inc(s_raw, 1)
                dve.tensor_tensor(vaug[:, t, :, 0:16], bank[3 * (t % 2) + 2][:].rearrange("p (h d) -> p h d", d=D),
                                  qkvb_sb[:, 2 * E:].rearrange("p (h d) -> p h d", d=D), ALU.add).then_inc(s_raw, 1)
                dve.wait_ge(s_raw, 2 * t + 2)

            def rope_cos(t):
                for f in range(2):
                    ins = dve.tensor_tensor(qkr[:, t // TB, f, :, t % TB, :].rearrange("p u (h d) -> p u h d", d=D),
                                            qkraw[:, t % 2, f].rearrange("p (u h) d -> p u h d", h=2),
                                            rope_sb[:, t % TB, f:f + 1, :].rearrange("p o (q d) -> p o q d", q=1)
                                            .broadcast_to([P, H // 2, 2, D]), ALU.mult)
                link(ins)

            def rope_sin(t):
                dve.wait_ge(s_rot, t + 1)
                for f in range(2):
                    q = qkr[:, t // TB, f, :, t % TB, :]
                    ins = dve.tensor_tensor(q, q, rot[:, f].rearrange("p (u h) d -> p u (h d)", h=2), ALU.add)
                ins.then_inc(s_rope, 1)

            for t in range(NT):
                if t + 2 < NT:
                    norm(t + 2)
                bias(t)
                if t >= 1:
                    rope_sin(t - 1)
                rope_cos(t)
            rope_sin(NT - 1)

            def high_parts(u):
                b, h0 = heads(u)
                if u >= 2:
                    dve.wait_ge(s_tr, u - 1)
                if u == 0:
                    dve.wait_ge(s_rope, NT)
                for f, st, again in ((0, qst, 16), (1, kst, 48)):
                    o = st[:, u % 2].rearrange("p t h (g c) -> p (t h) g c", c=16)
                    src = qkr[:, b, f, h0 // 2].rearrange("p t (h o d) -> p (t h) o d", o=1, d=D)
                    ins = dve.tensor_copy(o[:, :, 0:again // 16 + 1:again // 16, :], src.broadcast_to([P, 2 * TB, 2, D]))
                ins.then_inc(s_hi, 1)

            def evac(u):
                dve.wait_ge(s_tr, u + 1)
                if u >= 4:
                    dve.wait_ge(s_sc, 5 * (u - 3))
                dve.tensor_copy(kA[0:64, u % 4, :], TRK[0:64, :]).then_inc(s_ke, 1)

            def maxima(u, c):
                o = mneg[:, u % 2].rearrange("p (h i) -> p h i", i=TB)
                dve.wait_ge(s_mx, 6 * u + c + 1)
                if c == 0 and u >= 2:
                    dve.wait_ge(s_mt, u - 1)
                bk = MX[(6 * u + c) % 2]
                if c < 2:
                    w = P * (c + 1)
                    src, dst = bk[:, 0:2 * w].rearrange("p (h k) -> p h k", k=w), o[:, :, c]
                else:
                    i, h = c // 2 + 1, c % 2
                    src, dst = bk[:, 0:P * (i + 1)], o[:, h, i:i + 1]
                dve.tensor_reduce(dst, src, AX.X, ALU.max, negate=True).then_inc(s_red, 1)

            def ctx_evac(g):
                dve.wait_ge(s_pv, g + 1)
                if g >= 2:
                    dve.wait_ge(s_ct, g - 1)
                dve.tensor_copy(cT[:, g % 2, :], PVB[:]).then_inc(s_ce, 1)

            def ctx_norm(g):
                b, h0 = heads(2 * g)
                dve.wait_ge(s_ct, g + 1)
                v = MISC[:].rearrange("p (i h d) -> p i h d", i=TB, d=32)
                link(dve.reciprocal(rsum[:], v[:, :, :, 16]))
                dve.tensor_tensor(cx[:, b * TB:(b + 1) * TB, h0 * D:(h0 + 4) * D].rearrange("p i (h d) -> p i h d", d=D),
                                  v[:, :, :, 0:16], rsum[:].rearrange("p i (h o) -> p i h o", o=1).broadcast_to([P, TB, 4, D]),
                                  ALU.mult).then_inc(s_cx, 1)

            high_parts(0)
            high_parts(1)
            evac(0)
            for s in range(NP + 6):
                for c in range(6):
                    if s < NP:
                        maxima(s, c)
                    if c == 0 and s >= 6 and s % 2 == 0 and (s - 6) // 2 < NP // 2:
                        ctx_evac((s - 6) // 2)
                    if c == 2 and s + 1 < NP:
                        evac(s + 1)
                    if c == 3 and s + 2 < NP:
                        high_parts(s + 2)
                    if c == 4 and s >= 6 and s % 2 == 0 and (s - 6) // 2 < NP // 2:
                        ctx_norm((s - 6) // 2)

            def row_stats(src):
                for t in range(NT):
                    last = dve.bn_stats(stats[:, t, :], src[:, t, :])
                link(last)
                for t in range(NT):
                    last = dve.bn_aggr(mv[:, t, :], stats[:, t, :])
                link(last)
                rsqrt(rstd[:], mv[:, :, 1], (nwt[:, 0, :], nwt[:, 1, :]))

            def add_normed(t):
                link(dve.tensor_scalar(cx[:, t, :], cx[:, t, :], mv[:, t, 0:1], rstd[:, t:t + 1], ALU.subtract, ALU.mult))
                return dve.tensor_tensor(x_sb[:, t, :], x_sb[:, t, :], cx[:, t, :], ALU.add)

            for t in range(NT):
                dve.wait_ge(s_op, t + 1)
                ins = dve.tensor_tensor(cx[:, t, :], bank[2 + t % 4][:], outb_sb[:], ALU.add)
                ins.then_inc(s_a, 1)
            dve.wait_ge(s_a, NT)
            row_stats(cx)
            for t in range(NT):
                last = add_normed(t)
            link(last)
            row_stats(x_sb)
            for t in range(NT):
                dve.tensor_scalar(cx[:, t, :], x_sb[:, t, :], mv[:, t, 0:1], rstd[:, t:t + 1],
                                  ALU.subtract, ALU.mult).then_inc(s_h, 1)

            dve.wait_ge(s_rc, 96)
            dve.wait_ge(s_tanh, 1)
            link(dve.tensor_scalar(score[:], score[:], 0.5, 0.5, ALU.mult, ALU.add))
            link(dve.tensor_tensor(score[:], score[:], ebias_sb[:].rearrange("p (o e) -> p o e", o=1).broadcast_to([P, NT, NX]), ALU.add))
            mine = score[:].rearrange("p t (e o) -> p t e o", o=1).broadcast_to([P, NT, NX, NX])
            other = score[:].rearrange("p t (o f) -> p t o f", o=1).broadcast_to([P, NT, NX, NX])
            dve.tensor_tensor(above, other, mine, ALU.is_gt)
            link(dve.tensor_tensor(equal, other, mine, ALU.is_equal))
            link(dve.tensor_tensor(equal, equal, less_sb[:].rearrange("p (o e) f -> p o e f", o=1).broadcast_to([P, NT, NX, NX]), ALU.mult))
            link(dve.tensor_tensor(above, above, equal, ALU.add))
            link(dve.tensor_reduce(rank[:], above, AX.X, ALU.add))
            dve.tensor_scalar(chosen[:], rank[:], float(TOPK), None, ALU.is_lt).then_inc(s_ch, 1)

            def over_ranks(v):
                return v.rearrange("p t (o e) -> p t o e", o=1).broadcast_to([P, NT, TOPK, NX])

            link(dve.tensor_tensor(onehot[:], over_ranks(rank[:]),
                                   steps_sb[:, 0:TOPK].rearrange("p (o k q) -> p o k q", o=1, q=1).broadcast_to([P, NT, TOPK, NX]),
                                   ALU.is_equal))
            link(dve.tensor_tensor(pick[:], onehot[:], over_ranks(score[:]), ALU.mult))
            link(dve.tensor_reduce(wtop[:], pick[:], AX.X, ALU.add))
            link(dve.tensor_reduce(wden[:], wtop[:], AX.X, ALU.add))
            link(dve.tensor_scalar(wden[:], wden[:], 1e-20, None, ALU.add))
            link(dve.reciprocal(wden[:], wden[:]))
            dve.tensor_copy(pay[:, :, :, 0], tok_sb[:].rearrange("p (t o) -> p t o", o=1).broadcast_to([P, NT, TOPK]))
            dve.tensor_tensor(pay[:, :, :, 1].bitcast(F32), wtop[:],
                              wden[:].rearrange("p (t o) -> p t o", o=1).broadcast_to([P, NT, TOPK]), ALU.mult)
            link(dve.memset(before[:, 0, :], 0.0))
            dve.wait_ge(s_cnt, 1)
            total = bank[5][:, P:2 * P].rearrange("p (t e) -> p t e", e=NX)
            for t in range(NT):
                link(dve.tensor_tensor(before[:, t + 1, :], before[:, t, :], total[:, t, :], ALU.add))
            link(dve.tensor_scalar(tend[:], before[:, NT, :], 1.0 / P, None, ALU.mult))
            link(dve.tensor_tensor(cmp7[:], tend[:].rearrange("p (e o) -> p e o", o=1).broadcast_to([P, NX, 7]),
                                   steps_sb[:, 1:8].rearrange("p (o k) -> p o k", o=1).broadcast_to([P, NX, 7]), ALU.is_gt))
            link(dve.tensor_reduce(ntile[:], cmp7[:], AX.X, ALU.add))
            link(dve.tensor_scalar(ntile[:], ntile[:], 1.0, None, ALU.add))
            link(dve.tensor_tensor(tsum[:], less_sb[:], ntile[:].rearrange("p (o f) -> p o f", o=1).broadcast_to([P, NX, NX]), ALU.mult))
            link(dve.tensor_reduce(tfirst[:], tsum[:], AX.X, ALU.add))
            link(dve.tensor_tensor(tend[:], tfirst[:], ntile[:], ALU.add))
            link(dve.tensor_tensor(slot[:], before[:, 0:NT, :], bank[5][:, 0:P].rearrange("p (t e) -> p t e", e=NX), ALU.add))
            link(dve.tensor_scalar(tsum[:, 0, :], tfirst[:], float(P), None, ALU.mult))
            link(dve.tensor_tensor(slot[:], slot[:], tsum[:, 0:1, :].broadcast_to([P, NT, NX]), ALU.add))
            link(dve.tensor_tensor(pick[:], onehot[:], over_ranks(slot[:]), ALU.mult))
            link(dve.tensor_reduce(sl_f[:], pick[:], AX.X, ALU.add))
            link(dve.tensor_copy(sl_i[:, 0], sl_f[:]))
            link(dve.tensor_scalar(sl_i[:, 1], sl_i[:, 0], 7, None, ALU.logical_shift_right))
            link(dve.tensor_scalar(sl_i[:, 0], sl_i[:, 0], P - 1, 6, ALU.bitwise_and, ALU.logical_shift_left))
            dve.tensor_tensor(sl_i[:, 0], sl_i[:, 0], sl_i[:, 1], ALU.bitwise_or).then_inc(s_pay, 1)
            link(dve.tensor_tensor(owner, tfirst[:].rearrange("p (o e) -> p o e", o=1).broadcast_to([P, TT, NX]),
                                   steps_sb[:].rearrange("p (i o) -> p i o", o=1).broadcast_to([P, TT, NX]), ALU.is_le))
            link(dve.tensor_reduce(own[:], owner, AX.X, ALU.add))
            link(dve.tensor_copy(plan[:, 1, :], own[:]))
            link(dve.tensor_scalar(own[:], own[:], -1.0, None, ALU.add))
            link(dve.tensor_copy(plan[:, 0, :], own[:]))
            link(dve.tensor_scalar(plan[:, 0, :], plan[:, 0, :], RING - 1, None, ALU.bitwise_and))
            link(dve.tensor_scalar(plan[:, 0, :], plan[:, 0, :], float(WSLOT), None, ALU.mult))
            link(dve.tensor_copy(ends[:, 0:NX], tend[:]))
            link(dve.tensor_copy(ends[:, NX:NX + 1], tend[:, NX - 1:NX]))
            dve.tensor_scalar(ends[:, NX:NX + 1], ends[:, NX:NX + 1], 1, None, ALU.logical_shift_right).then_inc(s_plan, 1)

            for c in range(4):
                m, half = c // 2, c % 2
                dve.wait_ge(s_sth, c + 1)
                yy = y[:, c % 2, :]
                link(dve.scalar_tensor_tensor(out=yy, in0=yy, scalar=1.0, in1=bank[2 * (c % 2)][:], op0=ALU.add, op1=ALU.mult))
                dve.scalar_tensor_tensor(out=zs[:, m, half * 512:(half + 1) * 512], in0=bank[2 * (c % 2) + 1][:], scalar=0.5,
                                         in1=yy, op0=ALU.mult, op1=ALU.mult).then_inc(s_sz, 1)

            def inner(i, par):
                dve.wait_ge(s_th, i + 1)
                dve.scalar_tensor_tensor(out=act_z[:, par, :], in0=th[:, par, :], scalar=1.0, in1=bank[2 + par][:, 0:FI],
                                         op0=ALU.add, op1=ALU.mult).then_inc(s_az, 1)
                dve.wait_ge(s_az, i + 1)
                dve.scalar_tensor_tensor(out=z[:, par, :], in0=bank[2 + par][:, FI:2 * FI], scalar=0.5, in1=act_z[:, par, :],
                                         op0=ALU.mult, op1=ALU.mult).then_inc(s_z, 1)
                dve.wait_ge(s_tz, i + 1)
                dve.tensor_copy(zT[:, par].rearrange("p k q -> p (k q)"), bank[4 + par][:, 0:FI]).then_inc(s_zt, 1)

            dve.sem_inc(s_z, 1)
            n2 = dve.value_load(ends[0:1, NX:NX + 1], min_val=1, max_val=TT // 2 - 2)
            inner(0, 0)
            with dve.Fori(0, n2) as m:
                for r in range(2):
                    inner(2 * m + 1 + r, 1 - r)

            for b in range(B):
                dve.wait_ge(s_acc[b], 16)
            row_stats(cx)
            for t in range(NT):
                add_normed(t).then_inc(s_fin, 1)

        @block.tensor
        def _(pe):
            pe.wait_ge(s_const, 80)

            def turn_x(t):
                pe.wait_ge(s_xn, t + 1)
                if t >= 2:
                    pe.wait_ge(s_xT, t - 1)
                for k in range(KE):
                    mm = pe.transpose(bank[6 + t % 2][:, k * P:(k + 1) * P], xn[:, t % 2, k * P:(k + 1) * P], ident_sb[:])
                mm.then_inc(s_xtr, 1)

            turn_x(0)
            for t in range(NT):
                if t + 1 < NT:
                    turn_x(t + 1)
                pe.wait_ge(s_xT, t + 1)
                if t == 0:
                    pe.wait_ge(s_w, 16)
                if t >= 2:
                    pe.wait_ge(s_raw, 2 * (t - 1))
                for f in range(3):
                    for k in range(KE):
                        mm = pe.matmul(bank[3 * (t % 2) + f][:], xT[:, t % 2, k, :], qkvw_sb[:, k, f * E:(f + 1) * E],
                                       start=(k == 0), stop=(k == KE - 1))
                mm.then_inc(s_qkv, 1)
            pe.wait_ge(s_raw, 2 * NT)
            pe.wait_ge(s_idb, 1)

            def turn_q(u):
                pe.wait_ge(s_st, u + 1)
                if u >= 1:
                    pe.wait_ge(s_qe, u)
                for i in range(TB):
                    mm = pe.transpose(TRQ[:, i * P:(i + 1) * P], qst[:, u % 2, i].rearrange("p h c -> p (h c)").bitcast(F32), ident_sb[:])
                mm.then_inc(s_trq, 1)

            def turn_k(u):
                if u >= 1:
                    pe.wait_ge(s_ke, u)
                    pe.wait_ge(s_kf, u)
                for i in range(TB):
                    mm = pe.transpose(TRK[:, i * P:(i + 1) * P], kst[:, u % 2, i].rearrange("p h c -> p (h c)").bitcast(F32), ident_sb[:])
                mm.then_inc(s_tr, 1)

            def max_scores(u, c):
                if c == 0:
                    pe.wait_ge(s_qe, u + 1)
                    pe.wait_ge(s_ke, u + 1)
                    pe.wait_ge(s_kf, u + 1)
                q = qS[:, u % 4, :]
                n = 6 * u + c
                if n >= 2:
                    pe.wait_ge(s_red, n - 1)
                i = c if c < 2 else c // 2 + 1
                w = P * (i + 1)
                for h in ((0, 1) if c < 2 else (c % 2,)):
                    o = MX[n % 2][:, (h * w if c < 2 else 0):][:, 0:w]
                    pe.matmul(o, q[:, i * P:(i + 1) * P], (kA, kB)[h][:, u % 4, 0:w], start=True, stop=True)
                    mm = pe.matmul(o[:, w - P:w], identb[:], mask_sb[:], start=False, stop=True, skip_group_check=True)
                mm.then_inc(s_mx, 1)

            def turn_max(u):
                pe.wait_ge(s_red, 6 * (u + 1))
                if u >= 1:
                    pe.wait_ge(s_mc, u)
                if u >= 6:
                    pe.wait_ge(s_cx, (u - 4) // 2)
                pe.transpose(MISC[0:8, 0:P], mneg[:, u % 2, :].bitcast(F32), ident_sb[:]).then_inc(s_mt, 1)

            def scores(u, c):
                if c == 0:
                    pe.wait_ge(s_md[u % 4], 32 * (u // 4 + 1))
                n = 5 * u + c
                if n >= 2:
                    pe.wait_ge(s_ex, n - 1)
                for h, j, at in (((0, 0, 0),), ((1, 0, 0),), ((0, 1, 0), (0, 3, 384)),
                                 ((1, 1, 0), (1, 3, 384)), ((0, 2, 0), (1, 2, 256)))[c]:
                    mm = pe.matmul(ST[n % 2][:, at:at + S - j * P], (kA, kB)[h][:, u % 4, j * P:(j + 1) * P],
                                   qS[:, u % 4, j * P:], start=True, stop=True)
                mm.then_inc(s_sc, 1)

            def pv(g, j):
                b, h0 = heads(2 * g)
                if j == 0:
                    pe.wait_ge(s_zf, 2 * g + 2)
                    if g >= 1:
                        pe.wait_ge(s_ce, g)
                for h in range(4):
                    c, at = ((h % 2, 0), (2 + h % 2, 0), (4, 256 * (h % 2)), (2 + h % 2, 384))[j]
                    mm = pe.matmul(PVB[32 * h:32 * h + 32, j * P:], vaug[:, b * TB + j, h0 + h, :],
                                   probs[:, g % 2, h // 2, c, at:at + S - j * P], start=(j == 0), stop=True,
                                   skip_group_check=True)
                if j == TB - 1:
                    mm.then_inc(s_pv, 1)

            def turn_ctx(g):
                pe.wait_ge(s_ce, g + 1)
                pe.wait_ge(s_mc, min(2 * g + 6, NP))
                if g >= 1:
                    pe.wait_ge(s_cx, g)
                for i in range(TB):
                    mm = pe.transpose(MISC[:, i * P:(i + 1) * P], cT[:, g % 2, i * P:(i + 1) * P], ident_sb[:])
                mm.then_inc(s_ct, 1)

            turn_q(0)
            turn_k(0)
            for s in range(NP + 6):
                for c in range(6):
                    if 2 <= s < NP + 2 and c < 5:
                        scores(s - 2, c)
                    if s < NP:
                        max_scores(s, c)
                    if c == 0 and s + 1 < NP:
                        turn_q(s + 1)
                    if c == 1:
                        if s + 1 < NP:
                            turn_k(s + 1)
                        if 1 <= s <= NP:
                            turn_max(s - 1)
                    g = (s - 4) // 2
                    if c in (2, 4) and s >= 4 and g < NP // 2:
                        pv(g, 2 * (s % 2) + (c == 4))
                    if c == 3 and s >= 6 and s % 2 == 0 and (s - 6) // 2 < NP // 2:
                        turn_ctx((s - 6) // 2)
            pe.wait_ge(s_cx, NP // 2)
            pe.wait_ge(s_ow, 16)

            def turn_rows(t):
                if t >= 2:
                    pe.wait_ge(s_ctT, t - 1)
                for k in range(KE):
                    mm = pe.transpose(bank[t % 2][:, k * P:(k + 1) * P], cx[:, t, k * P:(k + 1) * P], ident_sb[:])
                mm.then_inc(s_ctr, 1)

            turn_rows(0)
            for t in range(NT):
                if t + 1 < NT:
                    turn_rows(t + 1)
                pe.wait_ge(s_ctT, t + 1)
                if t >= 4:
                    pe.wait_ge(s_a, t - 3)
                for k in range(KE):
                    mm = pe.matmul(bank[2 + t % 4][:], ctxT[:, t % 2, k, :], outw_sb[:, k, :], start=(k == 0), stop=(k == KE - 1))
                mm.then_inc(s_op, 1)
            for t in range(NT):
                pe.wait_ge(s_h, t + 1)
                if t >= 2:
                    pe.wait_ge(s_hT, t - 1)
                for k in range(KE):
                    mm = pe.transpose(bank[t % 2][:, k * P:(k + 1) * P], cx[:, t, k * P:(k + 1) * P], ident_sb[:])
                mm.then_inc(s_htr, 1)
            pe.wait_ge(s_rc, 96)
            pe.wait_ge(s_a, NT)
            for t in range(NT):
                pe.wait_ge(s_hT, t + 1)
                for k in range(KE):
                    mm = pe.matmul(bank[4][:, t * NX:(t + 1) * NX], hT[:, k, t * P:(t + 1) * P], gate_sb[:, k, :],
                                   start=(k == 0), stop=(k == KE - 1))
            mm.then_inc(s_lg, 1)
            pe.wait_ge(s_sw, 32)

            def shared_gu(c):
                m, n = c // 2, c % 2
                if c >= 2:
                    pe.wait_ge(s_sz, c - 1)
                for f in range(2):
                    for k in range(KE):
                        mm = pe.matmul(bank[2 * (c % 2) + f][:], sgu_sb[:, k, f * FI + m * P:f * FI + (m + 1) * P],
                                       hT[:, k, n * 512:(n + 1) * 512], start=(k == 0), stop=(k == KE - 1))
                mm.then_inc(s_sgu, 1)

            shared_gu(0)
            pe.wait_ge(s_ch, 1)
            ch = chosen[:].rearrange("p t e -> p (t e)")
            for f in range(2):
                mm = pe.matmul(bank[5][:, f * P:(f + 1) * P], tri_sb[:, f, :], ch, start=True, stop=True)
            mm.then_inc(s_cnt, 1)
            for c in range(1, 4):
                shared_gu(c)
            pe.wait_ge(s_sz, 4)
            for t in range(NT):
                if t >= 4:
                    pe.wait_ge(s_sy, t - 3)
                for k in range(KF):
                    mm = pe.matmul(bank[t % 4][:], zs[:, k, t * P:(t + 1) * P], sd_sb[:, k, :], start=(k == 0), stop=(k == KF - 1))
                mm.then_inc(s_sdn, 1)
            pe.wait_ge(s_sy, NT)

            def turn_gathered(par, at):
                pe.wait_ge(s_ga[par], at)
                for k in range(KE):
                    mm = pe.transpose(bank[par][:, k * P:(k + 1) * P], hg[:, par, k * P:(k + 1) * P], ident_sb[:])
                mm.then_inc(s_tx, 1)

            def gu(i, par, off):
                pe.wait_ge(s_he, i + 1)
                for k in range(KE):
                    mm = pe.matmul(bank[2 + par][:], hTt[:, par, k, :], ring[:, bass.ds(off + k * 2 * FI, 2 * FI)],
                                   start=(k == 0), stop=(k == KE - 1))
                mm.then_inc(s_gu, 1)

            def turn_z(i, par):
                pe.wait_ge(s_z, i + 2)
                for k in range(KF):
                    mm = pe.transpose(bank[4 + par][:, k * P:(k + 1) * P], z[:, par, k * P:(k + 1) * P], ident_sb[:])
                mm.then_inc(s_tz, 1)

            def down(j, par, off):
                pe.wait_ge(s_zt, j + 1)
                pe.wait_ge(s_ye, j + 2)
                for k in range(KF):
                    mm = pe.matmul(bank[6 + par][:], zT[:, par, k, :], ring[:, bass.ds(off + 2 * FI * KE + k * E, E)],
                                   start=(k == 0), stop=(k == KF - 1))
                mm.then_inc(s_dn, 1)

            pe.wait_ge(s_plan, 1)
            n2 = pe.value_load(ends[0:1, NX:NX + 1], min_val=1, max_val=TT // 2 - 2)

            def offset(i):
                return pe.value_load(plan[0:1, 0, bass.ds(i, 1)], min_val=0, max_val=(RING - 1) * WSLOT)

            turn_gathered(0, 16)
            pe.wait_ge(s_wr, 1)
            gu(0, 0, offset(0))
            turn_gathered(1, 16)
            turn_z(0, 0)
            with pe.Fori(0, n2) as m:
                for r in range(2):
                    i = 2 * m + 1 + r
                    pe.wait_ge(s_wr, pe.value_load(plan[0:1, 1, bass.ds(i, 1)], min_val=1, max_val=NX))
                    pe.wait_ge(s_z, i)
                    gu(i, 1 - r, offset(i))
                    turn_gathered(r, 16 * m + 32)
                    down(i - 1, r, offset(i - 1))
                    turn_z(i, 1 - r)
            down(2 * n2, 0, offset(2 * n2))


def _constants():
    import numpy as np
    half = D // 2
    inv = (np.float32(1.0) / np.float32(10000.0) ** (np.arange(half, dtype=np.float32) / np.float32(half))).astype(np.float32)
    ang = np.arange(S, dtype=np.float32)[:, None] * inv[None, :]
    cos, sin = np.cos(ang), np.sin(ang)
    cos, sin = np.concatenate([cos, cos], 1), np.concatenate([-sin, sin], 1)
    scale = np.float32(D ** -0.5)
    q = np.arange(P)
    fill = np.zeros((P, TT, 2), np.int32)
    fill[:, :, 0] = T + q[:, None]
    e = np.arange(NX)
    return {
        "ident": np.eye(P, dtype=np.float32),
        "mask": np.where(q[None, :] > q[:, None], MASKED_BITS, 0).astype(np.uint16),
        "tri": (np.stack([q[:, None] < q[None, :], np.ones((P, P), bool)], 1) * ONE_BITS).astype(np.uint16),
        "rope": np.stack([cos * scale, cos, sin * scale, sin], 1).astype(np.float32),
        "fill": fill.reshape(P * TT, 2),
        "tok": (q[:, None] + P * np.arange(NT)[None, :]).astype(np.int32),
        "less": (e[None, :] < e[:, None]).astype(np.float32),
        "steps": np.arange(TT, dtype=np.float32),
    }


def kernel(**inputs):
    import numpy as np
    import concourse.bacc as bacc
    from concourse.bass_utils import run_bass_kernel_spmd

    a = {k: np.asarray(v) for k, v in inputs.items()}

    def inner_layout(g, u):
        gu = np.concatenate([g, u], axis=-2).swapaxes(-1, -2)
        gu = gu.reshape(*gu.shape[:-2], KE, P, 2 * FI)
        return np.moveaxis(gu, -3, -2).reshape(*gu.shape[:-3], P, KE * 2 * FI)

    def down_layout(d):
        t = d.swapaxes(-1, -2)
        t = t.reshape(*t.shape[:-2], KF, P, E)
        return np.moveaxis(t, -3, -2).reshape(*t.shape[:-3], P, KF * E)

    arrays = {
        "x": a["L0_attn_hidden_states"].reshape(T, E),
        "qkv_w": a["L0_attn_qkv_w"],
        "qkv_b": a["L0_attn_qkv_b"],
        "out_w": a["L0_attn_out_w"],
        "out_b": a["L0_attn_out_b"],
        "gate": a["L0_ffn_gate_w"].T,
        "ebias": a["L0_ffn_bias"],
        "wg": np.concatenate([inner_layout(a["L0_ffn_Wg"], a["L0_ffn_Wu"]), down_layout(a["L0_ffn_Wd"])], axis=-1),
        "sg": np.concatenate([a["L0_ffn_Sg"], a["L0_ffn_Su"]], axis=0).T,
        "sd": a["L0_ffn_Sd"].T,
    }
    arrays = {k: np.ascontiguousarray(v) for k, v in {**arrays, **_constants()}.items()}
    nc = bacc.Bacc("TRN2", target_bir_lowering=False, num_devices=1)
    args = {k: nc.dram_tensor(f"in_{k}", v.shape, mybir.dt.from_np(v.dtype), kind="ExternalInput").ap() for k, v in arrays.items()}
    args["out"] = nc.dram_tensor("out_0", (T, E), F32, kind="ExternalOutput").ap()
    build(nc, **args)
    r = run_bass_kernel_spmd(nc, [{f"in_{k}": v for k, v in arrays.items()}], core_ids=[0])
    return r.results[0]["out_0"].reshape(B, S, E)
```

```python
from contextlib import ExitStack

import concourse.bass as bass
from concourse import mybir

F32 = mybir.dt.float32
F32R = mybir.dt.float32r
BF16 = mybir.dt.bfloat16
I32 = mybir.dt.int32
U32 = mybir.dt.uint32
ALU = mybir.AluOpType
ACT = mybir.ActivationFunctionType
AX = mybir.AxisListType

P = 128
B, S, E = 2, 512, 512
H, D = 32, 16
T = B * S
NT = T // P
TB = S // P
KE = E // P
NP = B * H // 2
STK = 64
NX, TOPK, FI = 16, 4, 256
KF = FI // P
MAXT = T * TOPK // P + NX - 1
TT = MAXT + 3
EPS = 1e-5
MASKED_BITS = 0xC782
ONE_BITS = 0x3F80
WSLOT = 3 * KE * FI
RING = 4


def build(nc, x, qkv_w, qkv_b, out_w, out_b, gate, ebias, wg, sg, sd,
          ident, mask, tri, rope, tok, less, steps, out):
    ctx = ExitStack()
    with ctx:
        def sb(name, shape, dt=F32):
            return ctx.enter_context(nc.sbuf_tensor(name, shape, dt))

        def sem(name):
            return ctx.enter_context(nc.semaphore(name))

        bank = [ctx.enter_context(nc.psum_tensor(f"bank{i}", [P, 512], F32)) for i in range(8)]

        ident_sb = sb("ident_sb", [P, P])
        identb = sb("identb", [P, P], BF16)
        mask_sb = sb("mask_sb", [P, P], BF16)
        rope_sb = sb("rope_sb", [P, TB, 4, D])
        qkvb_sb = sb("qkvb_sb", [P, 3 * E])
        outb_sb = sb("outb_sb", [P, E])
        x_sb = sb("x_sb", [P, NT, E])
        stats = sb("stats", [P, NT, 6])
        mv = sb("mv", [P, NT, 2])
        rstd = sb("rstd", [P, NT])
        nwt = sb("nwt", [P, 2, NT])
        work = sb("work", [P, 10240])
        qkvw_sb = work[:, 0:6144].rearrange("p (k n) -> p k n", k=KE)
        xn = work[:, 6144:7168].rearrange("p (r e) -> p r e", r=2)
        xT = work[:, 7168:8192].rearrange("p (r k q) -> p r k q", r=2, k=KE)
        qkraw = work[:, 8192:10240].rearrange("p (r f h d) -> p r f h d", r=2, f=2, h=H)
        probs = work[:].rearrange("p (r u c q) -> p r u c q", r=2, u=2, c=5)
        outw_sb = sb("outw_sb", [P, KE, E])
        rot = sb("rot", [P, 2, H, D])
        big = sb("big", [P, 16384])
        qkr = big[:, 0:8192].rearrange("p (b f u t c) -> p b f u t c", b=B, f=2, u=H // 2, t=TB)
        vaug = big[:, 8192:16384].rearrange("p (t h d) -> p t h d", t=NT, h=H)
        mneg = sb("mneg", [P, 2, 8], F32R)
        mT = sb("mT", [8, 2, P])
        cT = sb("cT", [P, 2, S])
        rsum = sb("rsum", [P, TB, 4])
        cx = sb("cx", [P, NT, E])

        s_const = sem("const_loaded")
        s_xin = [sem(f"x_loaded{b}") for b in range(B)]
        s_w = sem("qkv_weights_loaded")
        s_ow = sem("out_weights_loaded")
        s_idb = sem("identity_in_bf16")
        s_init = sem("buffers_initialised")
        dch = sem("vector_chain")
        pch = sem("pool_chain")
        s_xn = sem("xn_ready")
        s_xtr = sem("x_transposed")
        s_xT = sem("xT_ready")
        s_qkv = sem("qkv_done")
        s_raw = sem("qkv_evacuated")
        s_rot = sem("rope_sin_part_ready")
        s_rope = sem("rope_done")
        s_st = sem("stacks_ready")
        s_hi = sem("stacks_high_parts_ready")
        s_trq = sem("q_stacks_transposed")
        s_tr = sem("k_stacks_transposed")
        s_qe = sem("q_evacuated")
        s_ke = sem("kA_evacuated")
        s_kf = sem("kB_evacuated")
        s_mx = sem("max_scores_done")
        s_red = sem("max_reduced")
        s_mt = sem("max_transposed")
        s_mc = sem("max_rows_copied")
        s_md = [sem(f"max_rows_in_place{i}") for i in range(4)]
        s_sc = sem("scores_done")
        s_ex = sem("exp_done")
        s_zf = sem("masked_probs_zeroed")
        s_pv = sem("pv_done")
        s_ce = sem("ctx_evacuated")
        s_ct = sem("ctx_transposed")
        s_cx = sem("ctx_normalised")

        hT = work[:, 0:4096].rearrange("p (k t) -> p k t", k=KE)
        ctxT = work[:, 4096:5120].rearrange("p (r k q) -> p r k q", r=2, k=KE)
        sgu_sb = work[:, 5120:7168].rearrange("p (k n) -> p k n", k=KE)
        sd_sb = work[:, 7168:8192].rearrange("p (k n) -> p k n", k=KF)
        zs = work[:, 8192:10240].rearrange("p (k t) -> p k t", k=KF)
        ring = big[:, 0:RING * WSLOT]
        above = big[:, 12288:14336].rearrange("p (t e f) -> p t e f", t=NT, e=NX)
        equal = big[:, 14336:16384].rearrange("p (t e f) -> p t e f", t=NT, e=NX)
        gate_sb = sb("gate_sb", [P, KE, NX])
        ebias_sb = sb("ebias_sb", [P, NX])
        less_sb = sb("less_sb", [P, NX, NX])
        steps_sb = sb("steps_sb", [P, P])
        tri_sb = sb("tri_sb", [P, 2, P], BF16)
        score = sb("score", [P, NT, NX])
        rank = sb("rank", [P, NT, NX])
        chosen = sb("chosen", [P, NT, NX], BF16)
        onehot = sb("onehot", [P, NT, TOPK, NX])
        before = sb("before", [P, NT + 1, NX])
        slot = sb("slot", [P, NT, NX])
        cmp7 = sb("cmp7", [P, NX, 7])
        ntile = sb("ntile", [P, NX])
        tsum = sb("tsum", [P, NX, NX])
        tfirst = sb("tfirst", [P, NX])
        tend = sb("tend", [P, NX])
        owner = big[:, 12288:12288 + TT * NX].rearrange("p (i e) -> p i e", i=TT)
        own = sb("own", [P, TT])
        wtop = sb("wtop", [P, NT, TOPK])
        wden = sb("wden", [P, NT])
        sl_f = sb("sl_f", [P, NT, TOPK])
        sl_i = sb("sl_i", [P, 2, NT, TOPK], U32)
        sl_at = sb("sl_at", [P, 2, NT, TOPK])
        empty = sb("empty", [P, TT])
        tok_sb = sb("tok_sb", [P, NT + 1])
        plan = sb("plan", [P, 2, TT], I32)
        ends = sb("ends", [P, NX + 1], I32)
        table = sb("table", [P, TT, 2], I32)
        gidx = sb("gidx", [P, 2], U32)
        smeta = sb("smeta", [P, 2, 2], I32)
        loop = big[:, 12288:16384]
        hg = loop[:, 0:1024].rearrange("p (r e) -> p r e", r=2)
        hTt = loop[:, 1024:2048].rearrange("p (r k q) -> p r k q", r=2, k=KE)
        th = loop[:, 2048:2560].rearrange("p (r f) -> p r f", r=2)
        act_z = loop[:, 2560:3072].rearrange("p (r f) -> p r f", r=2)
        z = loop[:, 3072:3584].rearrange("p (r f) -> p r f", r=2)
        zT = loop[:, 3584:4096].rearrange("p (r k q) -> p r k q", r=2, k=KF)
        y = outw_sb[:, 0:2, :]
        sth = outw_sb[:, 2:4, :]
        stacks = ExitStack()
        qst, kst, qS, kA, kB = [stacks.enter_context(nc.sbuf_tensor(name, shape, F32R)) for name, shape in (
            ("qst", [P, 2, TB, 2, STK]), ("kst", [P, 2, TB, 2, STK]), ("qS", [P, 4, S]), ("kA", [P, 4, S]), ("kB", [P, 4, S]))]
        stacks.close()
        in_tile = sb("in_tile", [P, NT, TOPK, P])
        entry = sb("entry", [P, NT, TOPK, TT, 2])
        pick = sb("pick", [P, NT, TOPK, NX])
        h_rows = nc.dram_tensor("h_rows", (T + P, E), F32).ap()
        acc = nc.dram_tensor("acc_rows", (T + P, E), F32).ap()

        s_rc = sem("router_constants_loaded")
        s_ctr = sem("ctx_rows_turned")
        s_ctT = sem("ctxT_ready")
        s_op = sem("out_projected")
        s_a = sem("attention_rows_ready")
        s_h = sem("h_ready")
        s_hst = sem("h_stored")
        s_htr = sem("h_turned")
        s_hT = sem("hT_ready")
        s_lg = sem("logits_done")
        s_tanh = sem("router_tanh_done")
        s_ch = sem("chosen_ready")
        s_cnt = sem("counts_done")
        s_ent = sem("slot_entries_ready")
        s_sum = sem("slot_entries_summed")
        s_plan = sem("plan_ready")
        s_tab = sem("table_ready")
        s_sw = sem("shared_weights_loaded")
        s_sgu = sem("shared_gu_done")
        s_sth = sem("shared_tanh_done")
        s_sz = sem("shared_z_ready")
        s_sdn = sem("shared_down_done")
        s_sy = sem("shared_rows_ready")
        s_syst = [sem(f"shared_rows_stored{i}") for i in range(2)]
        s_wd = [sem(f"expert_weights_landed{i}") for i in range(RING)]
        s_wr = sem("expert_weights_ready")
        s_ga = [sem(f"rows_gathered{i}") for i in range(2)]
        s_tx = sem("rows_turned")
        s_he = sem("rows_evacuated")
        s_gu = sem("gu_done")
        s_th = sem("tanh_done")
        s_az = sem("silu_part_ready")
        s_z = sem("z_ready_plus_1")
        s_tz = sem("z_turned")
        s_zt = sem("zT_ready")
        s_dn = sem("down_done")
        s_ye = sem("y_ready_plus_3")
        s_ms = sem("slot_meta_ready")
        s_sca = sem("spare_row_stored_then_y_scattered")
        s_scd = sem("scatters_seen_plus_3")
        s_gi = sem("gathers_begun")
        s_ix = sem("gather_index_ready")
        s_mdone = sem("all_scattered")
        s_acc = [sem(f"acc_loaded{i}") for i in range(2)]
        s_fin = sem("rows_final")
        s_out = sem("out_stored")

        block = ctx.enter_context(nc.Block())

        TRQ, TRK, MX, ST, PVB, MISC = bank[0], bank[1], bank[2:4], bank[4:6], bank[6], bank[7]

        def heads(u):
            return u // (NP // B), 2 * (u % (NP // B))

        @block.sync
        def _(sp):
            for b in range(B):
                sp.dma_start(x_sb[:, b * TB:(b + 1) * TB, :],
                             x[b * S:(b + 1) * S, :].rearrange("(t p) e -> p t e", p=P)).then_inc(s_xin[b], 16)
            sp.dma_start(ident_sb[:], ident).then_inc(s_const, 16)
            sp.dma_start(mask_sb[:], mask.bitcast(BF16)).then_inc(s_const, 16)
            sp.dma_start(rope_sb[:], rope.rearrange("(t p) f d -> p t f d", p=P)).then_inc(s_const, 16)
            sp.dma_start(qkvw_sb[:], qkv_w.rearrange("(k p) n -> p k n", p=P)).then_inc(s_w, 16)
            sp.dma_start(qkvb_sb[:], qkv_b.rearrange("(o n) -> o n", o=1).broadcast_to([P, 3 * E])).then_inc(s_const, 16)
            sp.dma_start(outb_sb[:], out_b.rearrange("(o n) -> o n", o=1).broadcast_to([P, E])).then_inc(s_const, 16)
            sp.dma_start(outw_sb[:], out_w.rearrange("(k p) n -> p k n", p=P)).then_inc(s_ow, 16)
            for u in range(NP):
                sp.wait_ge(s_mc, u + 1)
                for h in range(2):
                    sp.dma_start(qS[64 * h + 32:64 * h + 33, u % 4, :].bitcast(F32).rearrange("o (i q) -> o i q", q=P),
                                 mT[4 * h:4 * h + 4, u % 2, :]).then_inc(s_md[u % 4], 16)
            sp.dma_start(gate_sb[:], gate.rearrange("(k p) n -> p k n", p=P)).then_inc(s_rc, 16)
            sp.dma_start(ebias_sb[:], ebias.rearrange("(o n) -> o n", o=1).broadcast_to([P, NX])).then_inc(s_rc, 16)
            sp.dma_start(less_sb[:], less.rearrange("(o e) f -> o e f", o=1).broadcast_to([P, NX, NX])).then_inc(s_rc, 16)
            sp.dma_start(steps_sb[:], steps.rearrange("(o n) -> o n", o=1).broadcast_to([P, P])).then_inc(s_rc, 16)
            sp.dma_start(tri_sb[:], tri.bitcast(BF16)).then_inc(s_rc, 16)
            sp.dma_start(tok_sb[:], tok).then_inc(s_rc, 16)
            sp.wait_ge(s_cx, NP // 2)
            sp.wait_ge(s_pv, NP // 2)
            sp.dma_start(sgu_sb[:], sg.rearrange("(k p) n -> p k n", p=P)).then_inc(s_sw, 16)
            sp.dma_start(sd_sb[:], sd.rearrange("(k p) n -> p k n", p=P)).then_inc(s_sw, 16)
            for e in range(RING):
                sp.dma_start(ring[:, e * WSLOT:(e + 1) * WSLOT], wg[e]).then_inc(s_wd[e], 16)
            for t in range(NT):
                sp.wait_ge(s_h, t + 1)
                sp.dma_start(h_rows[t * P:(t + 1) * P, :], cx[:, t, :]).then_inc(s_hst, 16)
            for t in range(NT):
                sp.wait_ge(s_sy, t + 1)
                sp.dma_start(acc[t * P:(t + 1) * P, :], y[:, t % 2, :]).then_inc(s_syst[t % 2], 16)
                if t == 0:
                    sp.dma_start(acc[T:T + P, :], y[:, 0, :]).then_inc(s_syst[0], 16)
            for e in range(RING):
                sp.wait_ge(s_wd[e], 16)
                sp.sem_inc(s_wr, 1)
            sp.wait_ge(s_plan, 1)
            for e in range(RING, NX):
                sp.wait_ge(s_dn, sp.value_load(ends[0:1, e - RING:e - RING + 1], min_val=1, max_val=MAXT))
                r = e % RING
                sp.dma_start(ring[:, r * WSLOT:(r + 1) * WSLOT], wg[e]).then_inc(s_wd[r], 16)
                sp.wait_ge(s_wd[r], 16 * (e // RING + 1))
                sp.sem_inc(s_wr, 1)
            sp.wait_ge(s_mdone, 1)
            for b in range(B):
                sp.dma_start(cx[:, b * TB:(b + 1) * TB, :],
                             acc[b * S:(b + 1) * S, :].rearrange("(t p) e -> p t e", p=P)).then_inc(s_acc[b], 16)
            for t in range(0, NT, 2):
                sp.wait_ge(s_fin, t + 2)
                sp.dma_start(out[t * P:(t + 2) * P, :].rearrange("(t p) e -> p t e", p=P),
                             x_sb[:, t:t + 2, :]).then_inc(s_out, 16)
            sp.wait_ge(s_out, 16 * NT // 2)

        @block.gpsimd
        def _(pool):
            n = [0]

            def link(ins):
                n[0] += 1
                ins.then_inc(pch, 1)
                pool.wait_ge(pch, n[0])

            pool.memset(qst[:].bitcast(U32), 0)
            pool.memset(kst[:].bitcast(U32), 0)
            link(pool.memset(kA[:].bitcast(U32), 0))
            link(pool.memset(kst[:, :, :, :, 32:33].bitcast(F32), 1.0))
            link(pool.memset(vaug[:, :, :, 17:32], 0.0))
            pool.memset(vaug[:, :, :, 16:17], 1.0)
            pool.memset(kB[:].bitcast(U32), 0).then_inc(s_init, 1)
            pool.wait_ge(s_const, 80)
            for t in range(NT):
                pool.wait_ge(s_raw, 2 * t + 1)
                if t >= 1:
                    pool.wait_ge(s_rope, t)
                raw = qkraw[:, t % 2]
                for half in range(2):
                    lo, hi = 8 * half, 8 * (1 - half)
                    for f in range(2):
                        ins = pool.tensor_tensor(
                            rot[:, f, :, lo:lo + 8], raw[:, f, :, hi:hi + 8],
                            rope_sb[:, t % TB, 2 + f:3 + f, lo:lo + 8].broadcast_to([P, H, 8]), ALU.mult)
                ins.then_inc(s_rot, 1)

            def low_parts(u):
                b, h0 = heads(u)
                pool.wait_ge(s_hi, u + 1)
                for f, st, low in ((0, qst, 48), (1, kst, 16)):
                    o = st[:, u % 2].rearrange("p t h c -> p (t h) c")
                    src = qkr[:, b, f, h0 // 2].rearrange("p t (h d) -> p (t h) d", d=D)
                    ins = pool.tensor_tensor(o[:, :, low:low + 16], src, o[:, :, 0:16].bitcast(F32), ALU.subtract)
                ins.then_inc(s_st, 1)

            def zero_masked(u):
                pb = probs[:, (u // 2) % 2, u % 2]
                for c, view in ((2, pb[:, 0:2, 0:128]),
                                (3, pb[:, 2, :].rearrange("p (d q) -> p d q", q=P)[:, 0:4:3, :]),
                                (4, pb[:, 3, :].rearrange("p (d q) -> p d q", q=P)[:, 0:4:3, :]),
                                (5, pb[:, 4, :].rearrange("p (d q) -> p d q", q=P)[:, 0:4:2, :])):
                    pool.wait_ge(s_ex, 5 * u + c)
                    pat = [[0, k] for k in view.shape[1:-1]] + [[1, P]]
                    ins = pool.affine_select(out=view, in_=view, compare_op=ALU.is_ge, fill=0.0, base=0,
                                             pattern=pat, channel_multiplier=-1)
                ins.then_inc(s_zf, 1)

            low_parts(0)
            for s in range(NP + 2):
                if s + 1 < NP:
                    low_parts(s + 1)
                if s - 2 >= 0:
                    zero_masked(s - 2)

            pool.wait_ge(s_h, 1)
            pool.dma_start(h_rows[T:T + P, :], cx[:, 0, :]).then_inc(s_sca, 16)

            def gather(i, par, after):
                if after is not None:
                    pool.wait_ge(s_tx, after)
                pool.tensor_copy(gidx[:, par:par + 1], table[:, bass.ds(i, 1), 0].bitcast(U32)).then_inc(s_ix, 1)
                pool.wait_ge(s_ix, i + 1)
                pool.sem_inc(s_gi, 1)
                pool.indirect_dma_start(hg[:, par, :], None, h_rows,
                                        bass.IndirectOffsetOnAxis(gidx[:, par:par + 1], 0)).then_inc(s_ga[par], 16)

            def meta(j, par):
                pool.tensor_copy(smeta[:, par, :], table[:, bass.ds(j, 1), :].rearrange("p o c -> p (o c)")).then_inc(s_ms, 1)

            def scatter(j, par):
                pool.wait_ge(s_ye, j + 4)
                pool.wait_ge(s_sca, 16 * j + 16)
                pool.sem_inc(s_scd, 1)
                pool.indirect_dma_start(acc, bass.IndirectOffsetOnAxis(smeta[:, par, 0:1].bitcast(U32), 0),
                                        y[:, par, :], None, compute_op=ALU.add).then_inc(s_sca, 16)

            pool.wait_ge(s_plan, 1)
            pool.wait_ge(s_tab, 1)
            pool.wait_ge(s_hst, 16 * NT)
            pool.wait_ge(s_sca, 16)
            pool.sem_inc(s_scd, 2)
            gather(0, 0, None)
            gather(1, 1, None)
            gather(2, 0, 1)
            pool.wait_ge(s_syst[0], 16 * (NT // 2 + 1))
            pool.wait_ge(s_syst[1], 16 * (NT // 2))
            n2 = pool.value_load(ends[0:1, NX:NX + 1], min_val=1, max_val=MAXT // 2)
            with pool.Fori(0, n2) as m:
                for r in range(2):
                    i = 2 * m + 1 + r
                    gather(i + 2, 1 - r, i + 1)
                    meta(i - 1, r)
                    scatter(i - 1, r)
            meta(2 * n2, 0)
            scatter(2 * n2, 0)
            pool.wait_ge(s_sca, 32 * n2 + 32)
            pool.sem_inc(s_mdone, 1)

        @block.scalar
        def _(act):
            for t in range(NT):
                act.wait_ge(s_xtr, t + 1)
                if t >= 2:
                    act.wait_ge(s_qkv, t - 1)
                act.activation(xT[:, t % 2].rearrange("p k q -> p (k q)"), bank[6 + t % 2][:], ACT.Copy).then_inc(s_xT, 1)
            act.wait_ge(s_init, 1)

            def q_evac(u):
                act.wait_ge(s_trq, u + 1)
                if u >= 4:
                    act.wait_ge(s_sc, 5 * (u - 3))
                act.activation(qS[:, u % 4, :], TRQ[:], ACT.Copy).then_inc(s_qe, 1)

            def kb_evac(u):
                act.wait_ge(s_tr, u + 1)
                if u >= 4:
                    act.wait_ge(s_sc, 5 * (u - 3))
                act.activation(kB[64:128, u % 4, :], TRK[64:128, :], ACT.Copy).then_inc(s_kf, 1)

            def max_rows(u):
                act.wait_ge(s_mt, u + 1)
                if u >= 2:
                    act.wait_ge(s_md[(u - 2) % 4], 32 * ((u - 2) // 4 + 1))
                act.activation(mT[:, u % 2, :], MISC[0:8, 0:P], ACT.Copy).then_inc(s_mc, 1)

            def exp(u, c):
                act.wait_ge(s_sc, 5 * u + c + 1)
                if c == 0 and u % 2 == 0 and u >= 4:
                    act.wait_ge(s_pv, u // 2 - 1)
                act.activation(probs[:, (u // 2) % 2, u % 2, c, :], ST[(5 * u + c) % 2][:], ACT.Exp).then_inc(s_ex, 1)

            q_evac(0)
            kb_evac(0)
            for s in range(NP + 2):
                for c in range(5):
                    if s >= 2:
                        exp(s - 2, c)
                    if c == 1 and s + 1 < NP:
                        q_evac(s + 1)
                    if c == 2 and 1 <= s <= NP:
                        max_rows(s - 1)
                    if c == 3 and s + 1 < NP:
                        kb_evac(s + 1)
            for t in range(NT):
                act.wait_ge(s_ctr, t + 1)
                if t >= 2:
                    act.wait_ge(s_op, t - 1)
                act.activation(ctxT[:, t % 2].rearrange("p k q -> p (k q)"), bank[t % 2][:], ACT.Copy).then_inc(s_ctT, 1)
            for b in range(B):
                for t in range(b * TB, (b + 1) * TB):
                    act.wait_ge(s_htr, t + 1)
                    act.activation(hT[:, :, t * P:(t + 1) * P], bank[t % 2][:].rearrange("p (k q) -> p k q", k=KE),
                                   ACT.Copy).then_inc(s_hT, 1)
                act.wait_ge(s_lg, b + 1)
                act.activation(score[:, b * TB:(b + 1) * TB, :].rearrange("p t e -> p (t e)"),
                               bank[6][:, b * TB * NX:(b + 1) * TB * NX], ACT.Tanh, scale=0.5).then_inc(s_tanh, 1)
                for c in range(2 * b, 2 * b + 2):
                    act.wait_ge(s_sgu, c + 1)
                    if c >= 2:
                        act.wait_ge(s_sz, c - 1)
                    act.activation(sth[:, c % 2, :], bank[2 + 2 * (c % 2)][:], ACT.Tanh, scale=0.5).then_inc(s_sth, 1)
            for t in range(NT):
                act.wait_ge(s_sdn, t + 1)
                if t >= 2:
                    act.wait_ge(s_syst[t % 2], 16 * (t // 2 + (t % 2 == 0)))
                act.activation(y[:, t % 2, :], bank[t % 4][:], ACT.Copy).then_inc(s_sy, 1)

            def rows_evac(i, par):
                act.wait_ge(s_tx, i + 1)
                act.activation(hTt[:, par].rearrange("p k q -> p (k q)"), bank[par][:], ACT.Copy).then_inc(s_he, 1)

            def tanh(i, par):
                act.wait_ge(s_gu, i + 1)
                act.wait_ge(s_z, i)
                act.activation(th[:, par, :], bank[2 + par][:, 0:FI], ACT.Tanh, scale=0.5).then_inc(s_th, 1)

            def y_evac(j, par):
                act.wait_ge(s_dn, j + 1)
                act.wait_ge(s_ms, j + 1)
                act.wait_ge(s_scd, j + 2)
                act.activation(y[:, par, :], bank[6 + par][:], ACT.Copy, scale=smeta[:, par, 1:2].bitcast(F32)).then_inc(s_ye, 1)

            act.wait_ge(s_syst[0], 16 * (NT // 2 + 1))
            act.wait_ge(s_syst[1], 16 * (NT // 2))
            act.sem_inc(s_ye, 3)
            act.wait_ge(s_plan, 1)
            n2 = act.value_load(ends[0:1, NX:NX + 1], min_val=1, max_val=MAXT // 2)
            rows_evac(0, 0)
            act.wait_ge(s_gu, 1)
            act.activation(th[:, 0, :], bank[2][:, 0:FI], ACT.Tanh, scale=0.5).then_inc(s_th, 1)
            rows_evac(1, 1)
            with act.Fori(0, n2) as m:
                for r in range(2):
                    i = 2 * m + 1 + r
                    tanh(i, 1 - r)
                    rows_evac(i + 1, r)
                    y_evac(i - 1, r)
            y_evac(2 * n2, 0)

        @block.vector
        def _(dve):
            n = [0]

            def link(ins):
                n[0] += 1
                ins.then_inc(dch, 1)
                dve.wait_ge(dch, n[0])

            def rsqrt(o, var, w):
                v, y = w
                link(dve.tensor_scalar(v, var, EPS, None, ALU.add))
                link(dve.tensor_scalar(y.bitcast(I32), v.bitcast(I32), 1, None, ALU.logical_shift_right))
                link(dve.tensor_scalar(y.bitcast(I32), y.bitcast(I32), -1.0, 1597463007.0, ALU.mult, ALU.add))
                for step in range(3):
                    link(dve.tensor_tensor(o, y, y, ALU.mult))
                    link(dve.scalar_tensor_tensor(out=o, in0=o, scalar=-0.5, in1=v, op0=ALU.mult, op1=ALU.mult))
                    to = o if step == 2 else y
                    link(dve.scalar_tensor_tensor(out=to, in0=o, scalar=1.5, in1=y, op0=ALU.add, op1=ALU.mult))

            def row_stats(src, b):
                tiles = slice(b * TB, (b + 1) * TB)
                for t in range(b * TB, (b + 1) * TB):
                    last = dve.bn_stats(stats[:, t, :], src[:, t, :])
                link(last)
                for t in range(b * TB, (b + 1) * TB):
                    last = dve.bn_aggr(mv[:, t, :], stats[:, t, :])
                link(last)
                rsqrt(rstd[:, tiles], mv[:, tiles, 1], (nwt[:, 0, tiles], nwt[:, 1, tiles]))

            def norm(t):
                if t >= 2:
                    dve.wait_ge(s_xtr, t - 1)
                dve.tensor_scalar(xn[:, t % 2, :], x_sb[:, t, :], mv[:, t, 0:1], rstd[:, t:t + 1],
                                  ALU.subtract, ALU.mult).then_inc(s_xn, 1)

            dve.wait_ge(s_xin[0], 16)
            row_stats(x_sb, 0)
            norm(0)
            norm(1)
            dve.wait_ge(s_xin[1], 16)
            row_stats(x_sb, 1)
            dve.wait_ge(s_const, 80)
            dve.tensor_copy(identb[:], ident_sb[:]).then_inc(s_idb, 1)
            dve.wait_ge(s_init, 1)

            def bias(t):
                dve.wait_ge(s_qkv, t + 1)
                raw = qkraw[:, t % 2]
                for f in range(2):
                    ins = dve.tensor_tensor(raw[:, f], bank[3 * (t % 2) + f][:], qkvb_sb[:, f * E:(f + 1) * E], ALU.add)
                ins.then_inc(s_raw, 1)
                dve.tensor_tensor(vaug[:, t, :, 0:16], bank[3 * (t % 2) + 2][:].rearrange("p (h d) -> p h d", d=D),
                                  qkvb_sb[:, 2 * E:].rearrange("p (h d) -> p h d", d=D), ALU.add).then_inc(s_raw, 1)
                dve.wait_ge(s_raw, 2 * t + 2)

            def rope_cos(t):
                for f in range(2):
                    ins = dve.tensor_tensor(qkr[:, t // TB, f, :, t % TB, :].rearrange("p u (h d) -> p u h d", d=D),
                                            qkraw[:, t % 2, f].rearrange("p (u h) d -> p u h d", h=2),
                                            rope_sb[:, t % TB, f:f + 1, :].rearrange("p o (q d) -> p o q d", q=1)
                                            .broadcast_to([P, H // 2, 2, D]), ALU.mult)
                link(ins)

            def rope_sin(t):
                dve.wait_ge(s_rot, t + 1)
                for f in range(2):
                    q = qkr[:, t // TB, f, :, t % TB, :]
                    ins = dve.tensor_tensor(q, q, rot[:, f].rearrange("p (u h) d -> p u (h d)", h=2), ALU.add)
                ins.then_inc(s_rope, 1)

            for t in range(NT):
                if t + 2 < NT:
                    norm(t + 2)
                bias(t)
                if t >= 1:
                    rope_sin(t - 1)
                rope_cos(t)
            rope_sin(NT - 1)

            def high_parts(u):
                b, h0 = heads(u)
                if u >= 2:
                    dve.wait_ge(s_tr, u - 1)
                if u == 0:
                    dve.wait_ge(s_rope, NT)
                for f, st, again in ((0, qst, 16), (1, kst, 48)):
                    o = st[:, u % 2].rearrange("p t h (g c) -> p (t h) g c", c=16)
                    src = qkr[:, b, f, h0 // 2].rearrange("p t (h o d) -> p (t h) o d", o=1, d=D)
                    ins = dve.tensor_copy(o[:, :, 0:again // 16 + 1:again // 16, :], src.broadcast_to([P, 2 * TB, 2, D]))
                ins.then_inc(s_hi, 1)

            def evac(u):
                dve.wait_ge(s_tr, u + 1)
                if u >= 4:
                    dve.wait_ge(s_sc, 5 * (u - 3))
                dve.tensor_copy(kA[0:64, u % 4, :], TRK[0:64, :]).then_inc(s_ke, 1)

            def maxima(u, c):
                o = mneg[:, u % 2].rearrange("p (h i) -> p h i", i=TB)
                dve.wait_ge(s_mx, 6 * u + c + 1)
                if c == 0 and u >= 2:
                    dve.wait_ge(s_mt, u - 1)
                bk = MX[(6 * u + c) % 2]
                if c < 2:
                    w = P * (c + 1)
                    src, dst = bk[:, 0:2 * w].rearrange("p (h k) -> p h k", k=w), o[:, :, c]
                else:
                    i, h = c // 2 + 1, c % 2
                    src, dst = bk[:, 0:P * (i + 1)], o[:, h, i:i + 1]
                dve.tensor_reduce(dst, src, AX.X, ALU.max, negate=True).then_inc(s_red, 1)

            def ctx_evac(g):
                dve.wait_ge(s_pv, g + 1)
                if g >= 2:
                    dve.wait_ge(s_ct, g - 1)
                dve.tensor_copy(cT[:, g % 2, :], PVB[:]).then_inc(s_ce, 1)

            def ctx_norm(g):
                b, h0 = heads(2 * g)
                dve.wait_ge(s_ct, g + 1)
                v = MISC[:].rearrange("p (i h d) -> p i h d", i=TB, d=32)
                link(dve.reciprocal(rsum[:], v[:, :, :, 16]))
                dve.tensor_tensor(cx[:, b * TB:(b + 1) * TB, h0 * D:(h0 + 4) * D].rearrange("p i (h d) -> p i h d", d=D),
                                  v[:, :, :, 0:16], rsum[:].rearrange("p i (h o) -> p i h o", o=1).broadcast_to([P, TB, 4, D]),
                                  ALU.mult).then_inc(s_cx, 1)

            high_parts(0)
            high_parts(1)
            evac(0)
            for s in range(NP + 6):
                for c in range(6):
                    if s < NP:
                        maxima(s, c)
                    if c == 0 and s >= 6 and s % 2 == 0 and (s - 6) // 2 < NP // 2:
                        ctx_evac((s - 6) // 2)
                    if c == 2 and s + 1 < NP:
                        evac(s + 1)
                    if c == 3 and s + 2 < NP:
                        high_parts(s + 2)
                    if c == 4 and s >= 6 and s % 2 == 0 and (s - 6) // 2 < NP // 2:
                        ctx_norm((s - 6) // 2)

            def add_normed(t):
                link(dve.tensor_scalar(cx[:, t, :], cx[:, t, :], mv[:, t, 0:1], rstd[:, t:t + 1], ALU.subtract, ALU.mult))
                return dve.tensor_tensor(x_sb[:, t, :], x_sb[:, t, :], cx[:, t, :], ALU.add)

            for b in range(B):
                tiles = range(b * TB, (b + 1) * TB)
                for t in tiles:
                    dve.wait_ge(s_op, t + 1)
                    dve.tensor_tensor(cx[:, t, :], bank[2 + t % 4][:], outb_sb[:], ALU.add).then_inc(s_a, 1)
                dve.wait_ge(s_a, TB * (b + 1))
                row_stats(cx, b)
                for t in tiles:
                    last = add_normed(t)
                link(last)
                row_stats(x_sb, b)
                for t in tiles:
                    dve.tensor_scalar(cx[:, t, :], x_sb[:, t, :], mv[:, t, 0:1], rstd[:, t:t + 1],
                                      ALU.subtract, ALU.mult).then_inc(s_h, 1)

            def shared_z(c):
                half, m = c // 2, c % 2
                g, u = bank[2 + 2 * (c % 2)][:], bank[3 + 2 * (c % 2)][:]
                dve.wait_ge(s_sth, c + 1)
                link(dve.scalar_tensor_tensor(out=sth[:, c % 2, :], in0=sth[:, c % 2, :], scalar=1.0, in1=g,
                                              op0=ALU.add, op1=ALU.mult))
                dve.scalar_tensor_tensor(out=zs[:, m, half * 512:(half + 1) * 512], in0=u, scalar=0.5,
                                         in1=sth[:, c % 2, :], op0=ALU.mult, op1=ALU.mult).then_inc(s_sz, 1)

            def rank_by_score(b):
                ts = slice(b * TB, (b + 1) * TB)
                shape = [P, TB, NX, NX]
                dve.wait_ge(s_tanh, b + 1)
                link(dve.tensor_scalar(score[:, ts], score[:, ts], 0.5, 0.5, ALU.mult, ALU.add))
                link(dve.tensor_tensor(score[:, ts], score[:, ts], ebias_sb[:].rearrange("p (o e) -> p o e", o=1)
                                       .broadcast_to([P, TB, NX]), ALU.add))
                mine = score[:, ts].rearrange("p t (e o) -> p t e o", o=1).broadcast_to(shape)
                other = score[:, ts].rearrange("p t (o f) -> p t o f", o=1).broadcast_to(shape)
                dve.tensor_tensor(above[:, ts], other, mine, ALU.is_gt)
                link(dve.tensor_tensor(equal[:, ts], other, mine, ALU.is_equal))
                link(dve.tensor_tensor(equal[:, ts], equal[:, ts], less_sb[:].rearrange("p (o e) f -> p o e f", o=1)
                                       .broadcast_to(shape), ALU.mult))
                link(dve.tensor_tensor(above[:, ts], above[:, ts], equal[:, ts], ALU.add))
                link(dve.tensor_reduce(rank[:, ts], above[:, ts], AX.X, ALU.add))
                dve.tensor_scalar(chosen[:, ts], rank[:, ts], float(TOPK), None, ALU.is_lt).then_inc(s_ch, 1)

            dve.wait_ge(s_rc, 96)
            shared_z(0)
            rank_by_score(0)
            shared_z(1)
            rank_by_score(1)

            def over_ranks(v):
                return v.rearrange("p t (o e) -> p t o e", o=1).broadcast_to([P, NT, TOPK, NX])

            link(dve.tensor_tensor(onehot[:], over_ranks(rank[:]),
                                   steps_sb[:, 0:TOPK].rearrange("p (o k q) -> p o k q", o=1, q=1).broadcast_to([P, NT, TOPK, NX]),
                                   ALU.is_equal))
            link(dve.tensor_tensor(pick[:], onehot[:], over_ranks(score[:]), ALU.mult))
            link(dve.tensor_reduce(wtop[:], pick[:], AX.X, ALU.add))
            link(dve.tensor_reduce(wden[:], wtop[:], AX.X, ALU.add))
            link(dve.tensor_scalar(wden[:], wden[:], 1e-20, None, ALU.add))
            link(dve.reciprocal(wden[:], wden[:]))
            dve.tensor_tensor(wtop[:], wtop[:], wden[:].rearrange("p (t o) -> p t o", o=1).broadcast_to([P, NT, TOPK]), ALU.mult)
            link(dve.memset(before[:, 0, :], 0.0))
            dve.wait_ge(s_cnt, 1)
            total = bank[7][:, P:2 * P].rearrange("p (t e) -> p t e", e=NX)
            for t in range(NT):
                link(dve.tensor_tensor(before[:, t + 1, :], before[:, t, :], total[:, t, :], ALU.add))
            link(dve.tensor_scalar(tend[:], before[:, NT, :], 1.0 / P, None, ALU.mult))
            link(dve.tensor_tensor(cmp7[:], tend[:].rearrange("p (e o) -> p e o", o=1).broadcast_to([P, NX, 7]),
                                   steps_sb[:, 1:8].rearrange("p (o k) -> p o k", o=1).broadcast_to([P, NX, 7]), ALU.is_gt))
            link(dve.tensor_reduce(ntile[:], cmp7[:], AX.X, ALU.add))
            link(dve.tensor_scalar(ntile[:], ntile[:], 1.0, None, ALU.add))
            link(dve.tensor_tensor(tsum[:], less_sb[:], ntile[:].rearrange("p (o f) -> p o f", o=1).broadcast_to([P, NX, NX]), ALU.mult))
            link(dve.tensor_reduce(tfirst[:], tsum[:], AX.X, ALU.add))
            link(dve.tensor_tensor(tend[:], tfirst[:], ntile[:], ALU.add))
            link(dve.tensor_tensor(slot[:], before[:, 0:NT, :], bank[7][:, 0:P].rearrange("p (t e) -> p t e", e=NX), ALU.add))
            link(dve.tensor_scalar(tsum[:, 0, :], tfirst[:], float(P), None, ALU.mult))
            link(dve.tensor_tensor(slot[:], slot[:], tsum[:, 0:1, :].broadcast_to([P, NT, NX]), ALU.add))
            link(dve.tensor_tensor(pick[:], onehot[:], over_ranks(slot[:]), ALU.mult))
            link(dve.tensor_reduce(sl_f[:], pick[:], AX.X, ALU.add))
            link(dve.tensor_copy(sl_i[:, 0], sl_f[:]))
            link(dve.tensor_scalar(sl_i[:, 1], sl_i[:, 0], P.bit_length() - 1, None, ALU.logical_shift_right))
            link(dve.tensor_scalar(sl_i[:, 0], sl_i[:, 0], P - 1, None, ALU.bitwise_and))
            link(dve.tensor_copy(sl_at[:], sl_i[:]))
            shared_z(2)
            for b in range(B):
                for t in range(b * TB, (b + 1) * TB):
                    wide = [P, TOPK, TT]
                    dve.tensor_tensor(in_tile[:, t], steps_sb[:].rearrange("p (o q) -> p o q", o=1).broadcast_to([P, TOPK, P]),
                                      sl_at[:, 0, t].rearrange("p (k o) -> p k o", o=1).broadcast_to([P, TOPK, P]), ALU.is_equal)
                    last = dve.tensor_tensor(entry[:, t, :, :, 0], steps_sb[:, 0:TT].rearrange("p (o q) -> p o q", o=1).broadcast_to(wide),
                                             sl_at[:, 1, t].rearrange("p (k o) -> p k o", o=1).broadcast_to(wide), ALU.is_equal)
                link(last)
                for t in range(b * TB, (b + 1) * TB):
                    last = dve.tensor_tensor(entry[:, t, :, :, 1], entry[:, t, :, :, 0],
                                             wtop[:, t].rearrange("p (k o) -> p k o", o=1).broadcast_to(wide), ALU.mult)
                link(last)
                for t in range(b * TB, (b + 1) * TB):
                    last = dve.tensor_scalar(entry[:, t, :, :, 0], entry[:, t, :, :, 0], tok_sb[:, t:t + 1], None, ALU.mult)
                last.then_inc(s_ent, 1)
                if b == 0:
                    shared_z(3)
            link(dve.tensor_tensor(owner, tfirst[:].rearrange("p (o e) -> p o e", o=1).broadcast_to([P, TT, NX]),
                                   steps_sb[:, 0:TT].rearrange("p (i o) -> p i o", o=1).broadcast_to([P, TT, NX]), ALU.is_le))
            link(dve.tensor_reduce(own[:], owner, AX.X, ALU.add))
            link(dve.tensor_copy(plan[:, 1, :], own[:]))
            link(dve.tensor_scalar(own[:], own[:], -1.0, None, ALU.add))
            link(dve.tensor_copy(plan[:, 0, :], own[:]))
            link(dve.tensor_scalar(plan[:, 0, :], plan[:, 0, :], RING - 1, None, ALU.bitwise_and))
            link(dve.tensor_scalar(plan[:, 0, :], plan[:, 0, :], float(WSLOT), None, ALU.mult))
            link(dve.tensor_copy(ends[:, 0:NX], tend[:]))
            link(dve.tensor_copy(ends[:, NX:NX + 1], tend[:, NX - 1:NX]))
            dve.tensor_scalar(ends[:, NX:NX + 1], ends[:, NX:NX + 1], 1, None, ALU.logical_shift_right).then_inc(s_plan, 1)

            dve.wait_ge(s_sum, 1)
            summed = bank[6][:, 0:2 * TT].rearrange("p (i c) -> p i c", c=2)
            dve.tensor_copy(table[:, :, 1].bitcast(F32), summed[:, :, 1])
            link(dve.tensor_scalar(empty[:], summed[:, :, 0], 0.0, tok_sb[:, NT:NT + 1], ALU.is_equal, ALU.mult))
            dve.scalar_tensor_tensor(out=table[:, :, 0], in0=summed[:, :, 0], scalar=-1.0, in1=empty[:],
                                     op0=ALU.add, op1=ALU.add).then_inc(s_tab, 1)

            def inner(i, par):
                dve.wait_ge(s_th, i + 1)
                dve.scalar_tensor_tensor(out=act_z[:, par, :], in0=th[:, par, :], scalar=1.0, in1=bank[2 + par][:, 0:FI],
                                         op0=ALU.add, op1=ALU.mult).then_inc(s_az, 1)
                dve.wait_ge(s_az, i + 1)
                dve.scalar_tensor_tensor(out=z[:, par, :], in0=bank[2 + par][:, FI:2 * FI], scalar=0.5, in1=act_z[:, par, :],
                                         op0=ALU.mult, op1=ALU.mult).then_inc(s_z, 1)
                dve.wait_ge(s_tz, i + 1)
                dve.tensor_copy(zT[:, par].rearrange("p k q -> p (k q)"), bank[4 + par][:, 0:FI]).then_inc(s_zt, 1)

            dve.sem_inc(s_z, 1)
            n2 = dve.value_load(ends[0:1, NX:NX + 1], min_val=1, max_val=MAXT // 2)
            inner(0, 0)
            with dve.Fori(0, n2) as m:
                for r in range(2):
                    inner(2 * m + 1 + r, 1 - r)

            for b in range(B):
                dve.wait_ge(s_acc[b], 16)
                row_stats(cx, b)
                for t in range(b * TB, (b + 1) * TB):
                    add_normed(t).then_inc(s_fin, 1)

        @block.tensor
        def _(pe):
            pe.wait_ge(s_const, 80)

            def turn_x(t):
                pe.wait_ge(s_xn, t + 1)
                if t >= 2:
                    pe.wait_ge(s_xT, t - 1)
                for k in range(KE):
                    mm = pe.transpose(bank[6 + t % 2][:, k * P:(k + 1) * P], xn[:, t % 2, k * P:(k + 1) * P], ident_sb[:])
                mm.then_inc(s_xtr, 1)

            turn_x(0)
            for t in range(NT):
                if t + 1 < NT:
                    turn_x(t + 1)
                pe.wait_ge(s_xT, t + 1)
                if t == 0:
                    pe.wait_ge(s_w, 16)
                if t >= 2:
                    pe.wait_ge(s_raw, 2 * (t - 1))
                for f in range(3):
                    for k in range(KE):
                        mm = pe.matmul(bank[3 * (t % 2) + f][:], xT[:, t % 2, k, :], qkvw_sb[:, k, f * E:(f + 1) * E],
                                       start=(k == 0), stop=(k == KE - 1))
                mm.then_inc(s_qkv, 1)
            pe.wait_ge(s_raw, 2 * NT)
            pe.wait_ge(s_idb, 1)

            def turn_q(u):
                pe.wait_ge(s_st, u + 1)
                if u >= 1:
                    pe.wait_ge(s_qe, u)
                for i in range(TB):
                    mm = pe.transpose(TRQ[:, i * P:(i + 1) * P], qst[:, u % 2, i].rearrange("p h c -> p (h c)").bitcast(F32), ident_sb[:])
                mm.then_inc(s_trq, 1)

            def turn_k(u):
                if u >= 1:
                    pe.wait_ge(s_ke, u)
                    pe.wait_ge(s_kf, u)
                for i in range(TB):
                    mm = pe.transpose(TRK[:, i * P:(i + 1) * P], kst[:, u % 2, i].rearrange("p h c -> p (h c)").bitcast(F32), ident_sb[:])
                mm.then_inc(s_tr, 1)

            def max_scores(u, c):
                if c == 0:
                    pe.wait_ge(s_qe, u + 1)
                    pe.wait_ge(s_ke, u + 1)
                    pe.wait_ge(s_kf, u + 1)
                q = qS[:, u % 4, :]
                n = 6 * u + c
                if n >= 2:
                    pe.wait_ge(s_red, n - 1)
                i = c if c < 2 else c // 2 + 1
                w = P * (i + 1)
                for h in ((0, 1) if c < 2 else (c % 2,)):
                    o = MX[n % 2][:, (h * w if c < 2 else 0):][:, 0:w]
                    pe.matmul(o, q[:, i * P:(i + 1) * P], (kA, kB)[h][:, u % 4, 0:w], start=True, stop=True)
                    mm = pe.matmul(o[:, w - P:w], identb[:], mask_sb[:], start=False, stop=True, skip_group_check=True)
                mm.then_inc(s_mx, 1)

            def turn_max(u):
                pe.wait_ge(s_red, 6 * (u + 1))
                if u >= 1:
                    pe.wait_ge(s_mc, u)
                if u >= 6:
                    pe.wait_ge(s_cx, (u - 4) // 2)
                pe.transpose(MISC[0:8, 0:P], mneg[:, u % 2, :].bitcast(F32), ident_sb[:]).then_inc(s_mt, 1)

            def scores(u, c):
                if c == 0:
                    pe.wait_ge(s_md[u % 4], 32 * (u // 4 + 1))
                n = 5 * u + c
                if n >= 2:
                    pe.wait_ge(s_ex, n - 1)
                for h, j, at in (((0, 0, 0),), ((1, 0, 0),), ((0, 1, 0), (0, 3, 384)),
                                 ((1, 1, 0), (1, 3, 384)), ((0, 2, 0), (1, 2, 256)))[c]:
                    mm = pe.matmul(ST[n % 2][:, at:at + S - j * P], (kA, kB)[h][:, u % 4, j * P:(j + 1) * P],
                                   qS[:, u % 4, j * P:], start=True, stop=True)
                mm.then_inc(s_sc, 1)

            def pv(g, j):
                b, h0 = heads(2 * g)
                if j == 0:
                    pe.wait_ge(s_zf, 2 * g + 2)
                    if g >= 1:
                        pe.wait_ge(s_ce, g)
                for h in range(4):
                    c, at = ((h % 2, 0), (2 + h % 2, 0), (4, 256 * (h % 2)), (2 + h % 2, 384))[j]
                    mm = pe.matmul(PVB[32 * h:32 * h + 32, j * P:], vaug[:, b * TB + j, h0 + h, :],
                                   probs[:, g % 2, h // 2, c, at:at + S - j * P], start=(j == 0), stop=True,
                                   skip_group_check=True)
                if j == TB - 1:
                    mm.then_inc(s_pv, 1)

            def turn_ctx(g):
                pe.wait_ge(s_ce, g + 1)
                pe.wait_ge(s_mc, min(2 * g + 6, NP))
                if g >= 1:
                    pe.wait_ge(s_cx, g)
                for i in range(TB):
                    mm = pe.transpose(MISC[:, i * P:(i + 1) * P], cT[:, g % 2, i * P:(i + 1) * P], ident_sb[:])
                mm.then_inc(s_ct, 1)

            turn_q(0)
            turn_k(0)
            for s in range(NP + 6):
                for c in range(6):
                    if 2 <= s < NP + 2 and c < 5:
                        scores(s - 2, c)
                    if s < NP:
                        max_scores(s, c)
                    if c == 0 and s + 1 < NP:
                        turn_q(s + 1)
                    if c == 1:
                        if s + 1 < NP:
                            turn_k(s + 1)
                        if 1 <= s <= NP:
                            turn_max(s - 1)
                    g = (s - 4) // 2
                    if c in (2, 4) and s >= 4 and g < NP // 2:
                        pv(g, 2 * (s % 2) + (c == 4))
                    if c == 3 and s >= 6 and s % 2 == 0 and (s - 6) // 2 < NP // 2:
                        turn_ctx((s - 6) // 2)
            pe.wait_ge(s_cx, NP // 2)
            pe.wait_ge(s_ow, 16)

            def turn_rows(t):
                if t >= 2:
                    pe.wait_ge(s_ctT, t - 1)
                for k in range(KE):
                    mm = pe.transpose(bank[t % 2][:, k * P:(k + 1) * P], cx[:, t, k * P:(k + 1) * P], ident_sb[:])
                mm.then_inc(s_ctr, 1)

            turn_rows(0)
            for t in range(NT):
                if t + 1 < NT:
                    turn_rows(t + 1)
                pe.wait_ge(s_ctT, t + 1)
                if t >= 4:
                    pe.wait_ge(s_a, t - 3)
                for k in range(KE):
                    mm = pe.matmul(bank[2 + t % 4][:], ctxT[:, t % 2, k, :], outw_sb[:, k, :], start=(k == 0), stop=(k == KE - 1))
                mm.then_inc(s_op, 1)
            def turn_h(t):
                pe.wait_ge(s_h, t + 1)
                if t >= 2:
                    pe.wait_ge(s_hT, t - 1)
                for k in range(KE):
                    mm = pe.transpose(bank[t % 2][:, k * P:(k + 1) * P], cx[:, t, k * P:(k + 1) * P], ident_sb[:])
                mm.then_inc(s_htr, 1)

            def logits(t):
                pe.wait_ge(s_hT, t + 1)
                for k in range(KE):
                    mm = pe.matmul(bank[6][:, t * NX:(t + 1) * NX], hT[:, k, t * P:(t + 1) * P], gate_sb[:, k, :],
                                   start=(k == 0), stop=(k == KE - 1))
                return mm

            def shared_gu(c):
                n, m = c // 2, c % 2
                if c >= 2:
                    pe.wait_ge(s_sz, c - 1)
                for f in range(2):
                    for k in range(KE):
                        mm = pe.matmul(bank[2 + 2 * (c % 2) + f][:], sgu_sb[:, k, f * FI + m * P:f * FI + (m + 1) * P],
                                       hT[:, k, n * 512:(n + 1) * 512], start=(k == 0), stop=(k == KE - 1))
                mm.then_inc(s_sgu, 1)

            pe.wait_ge(s_rc, 96)
            for b in range(B):
                for t in range(b * TB, (b + 1) * TB):
                    turn_h(t)
                for t in range(b * TB, (b + 1) * TB):
                    mm = logits(t)
                mm.then_inc(s_lg, 1)
                if b == 0:
                    pe.wait_ge(s_sw, 32)
                    pe.wait_ge(s_a, NT)
                shared_gu(2 * b)
                if b == B - 1:
                    pe.wait_ge(s_ch, B)
                    ch = chosen[:].rearrange("p t e -> p (t e)")
                    for f in range(2):
                        mm = pe.matmul(bank[7][:, f * P:(f + 1) * P], tri_sb[:, f, :], ch, start=True, stop=True)
                    mm.then_inc(s_cnt, 1)
                shared_gu(2 * b + 1)
            for t in range(NT):
                if t % TB == 0:
                    pe.wait_ge(s_sz, 2 * (t // TB + 1))
                if t == 2:
                    pe.wait_ge(s_sz, 3)
                if t >= 4:
                    pe.wait_ge(s_sy, t - 3)
                for k in range(KF):
                    mm = pe.matmul(bank[t % 4][:], zs[:, k, t * P:(t + 1) * P], sd_sb[:, k, :], start=(k == 0), stop=(k == KF - 1))
                mm.then_inc(s_sdn, 1)
            for t in range(NT):
                if t % TB == 0:
                    pe.wait_ge(s_ent, t // TB + 1)
                for k in range(TOPK):
                    mm = pe.matmul(bank[6][:, 0:2 * TT], in_tile[:, t, k, :], entry[:, t, k].rearrange("p i c -> p (i c)"),
                                   start=(t == 0 and k == 0), stop=(t == NT - 1 and k == TOPK - 1))
            mm.then_inc(s_sum, 1)
            pe.wait_ge(s_sy, NT)

            def turn_gathered(par, at):
                pe.wait_ge(s_ga[par], at)
                for k in range(KE):
                    mm = pe.transpose(bank[par][:, k * P:(k + 1) * P], hg[:, par, k * P:(k + 1) * P], ident_sb[:])
                mm.then_inc(s_tx, 1)

            def gu(i, par, off):
                pe.wait_ge(s_he, i + 1)
                for k in range(KE):
                    mm = pe.matmul(bank[2 + par][:], hTt[:, par, k, :], ring[:, bass.ds(off + k * 2 * FI, 2 * FI)],
                                   start=(k == 0), stop=(k == KE - 1))
                mm.then_inc(s_gu, 1)

            def turn_z(i, par):
                pe.wait_ge(s_z, i + 2)
                for k in range(KF):
                    mm = pe.transpose(bank[4 + par][:, k * P:(k + 1) * P], z[:, par, k * P:(k + 1) * P], ident_sb[:])
                mm.then_inc(s_tz, 1)

            def down(j, par, off):
                pe.wait_ge(s_zt, j + 1)
                pe.wait_ge(s_ye, j + 2)
                for k in range(KF):
                    mm = pe.matmul(bank[6 + par][:], zT[:, par, k, :], ring[:, bass.ds(off + 2 * FI * KE + k * E, E)],
                                   start=(k == 0), stop=(k == KF - 1))
                mm.then_inc(s_dn, 1)

            pe.wait_ge(s_plan, 1)
            n2 = pe.value_load(ends[0:1, NX:NX + 1], min_val=1, max_val=MAXT // 2)

            at = [pe.alloc_register(f"weights_at{i}") for i in range(2)]

            def load_offset(i, par):
                pe.reg_load(at[par], plan[0:1, 0, bass.ds(i, 1)])

            def offset(par):
                return pe.snap(at[par], min_val=0, max_val=(RING - 1) * WSLOT)

            load_offset(0, 0)
            load_offset(1, 1)
            turn_gathered(0, 16)
            first = offset(0)
            pe.wait_ge(s_wr, 1)
            gu(0, 0, first)
            turn_gathered(1, 16)
            pe.wait_ge(s_wr, pe.value_load(plan[0:1, 1, 1:2], min_val=1, max_val=NX))
            turn_z(0, 0)
            with pe.Fori(0, n2) as m:
                for r in range(2):
                    i = 2 * m + 1 + r
                    here, before_it = offset(1 - r), offset(r)
                    pe.wait_ge(s_z, i)
                    gu(i, 1 - r, here)
                    turn_gathered(r, 16 * m + 32)
                    down(i - 1, r, before_it)
                    load_offset(i + 1, r)
                    pe.wait_ge(s_wr, pe.value_load(plan[0:1, 1, bass.ds(i + 1, 1)], min_val=1, max_val=NX))
                    turn_z(i, 1 - r)
            down(2 * n2, 0, offset(0))


def _constants():
    import numpy as np
    half = D // 2
    inv = (np.float32(1.0) / np.float32(10000.0) ** (np.arange(half, dtype=np.float32) / np.float32(half))).astype(np.float32)
    ang = np.arange(S, dtype=np.float32)[:, None] * inv[None, :]
    cos, sin = np.cos(ang), np.sin(ang)
    cos, sin = np.concatenate([cos, cos], 1), np.concatenate([-sin, sin], 1)
    scale = np.float32(D ** -0.5)
    q = np.arange(P)
    e = np.arange(NX)
    return {
        "ident": np.eye(P, dtype=np.float32),
        "mask": np.where(q[None, :] > q[:, None], MASKED_BITS, 0).astype(np.uint16),
        "tri": (np.stack([q[:, None] < q[None, :], np.ones((P, P), bool)], 1) * ONE_BITS).astype(np.uint16),
        "rope": np.stack([cos * scale, cos, sin * scale, sin], 1).astype(np.float32),
        "tok": (q[:, None] + P * np.arange(NT + 1)[None, :] + 1).astype(np.float32),
        "less": (e[None, :] < e[:, None]).astype(np.float32),
        "steps": np.arange(P, dtype=np.float32),
    }


def kernel(**inputs):
    import numpy as np
    import concourse.bacc as bacc
    from concourse.bass_utils import run_bass_kernel_spmd

    a = {k: np.asarray(v) for k, v in inputs.items()}

    def inner_layout(g, u):
        gu = np.concatenate([g, u], axis=-2).swapaxes(-1, -2)
        gu = gu.reshape(*gu.shape[:-2], KE, P, 2 * FI)
        return np.moveaxis(gu, -3, -2).reshape(*gu.shape[:-3], P, KE * 2 * FI)

    def down_layout(d):
        t = d.swapaxes(-1, -2)
        t = t.reshape(*t.shape[:-2], KF, P, E)
        return np.moveaxis(t, -3, -2).reshape(*t.shape[:-3], P, KF * E)

    arrays = {
        "x": a["L0_attn_hidden_states"].reshape(T, E),
        "qkv_w": a["L0_attn_qkv_w"],
        "qkv_b": a["L0_attn_qkv_b"],
        "out_w": a["L0_attn_out_w"],
        "out_b": a["L0_attn_out_b"],
        "gate": a["L0_ffn_gate_w"].T,
        "ebias": a["L0_ffn_bias"],
        "wg": np.concatenate([inner_layout(a["L0_ffn_Wg"], a["L0_ffn_Wu"]), down_layout(a["L0_ffn_Wd"])], axis=-1),
        "sg": np.concatenate([a["L0_ffn_Sg"], a["L0_ffn_Su"]], axis=0).T,
        "sd": a["L0_ffn_Sd"].T,
    }
    arrays = {k: np.ascontiguousarray(v) for k, v in {**arrays, **_constants()}.items()}
    nc = bacc.Bacc("TRN2", target_bir_lowering=False, num_devices=1)
    args = {k: nc.dram_tensor(f"in_{k}", v.shape, mybir.dt.from_np(v.dtype), kind="ExternalInput").ap() for k, v in arrays.items()}
    args["out"] = nc.dram_tensor("out_0", (T, E), F32, kind="ExternalOutput").ap()
    build(nc, **args)
    r = run_bass_kernel_spmd(nc, [{f"in_{k}": v for k, v in arrays.items()}], core_ids=[0])
    return r.results[0]["out_0"].reshape(B, S, E)
```
